# Optimizing a Trainium2 kernel written in Bass

```python
import numpy as np
import jax
import jax.numpy as jnp

def _softmax(x, axis=-1):
    return jax.nn.softmax(x, axis=axis)

def _gelu(x):
    return jax.nn.gelu(x, approximate=True)

def _silu(x):
    return jax.nn.silu(x)

def _sigmoid(x):
    return jax.nn.sigmoid(x)

def _layernorm(x, axis=-1, eps=1e-05):
    m = jnp.mean(x, axis=axis, keepdims=True)
    v = jnp.var(x, axis=axis, keepdims=True)
    return (x - m) / jnp.sqrt(v + eps)

def _scatter_add(tgt, idx, src, axis=0):
    return tgt.at[idx].add(src)

def _segment_sum(src, seg, n):
    return jax.ops.segment_sum(src, seg, n)
kernel_name = 'mk_decoder_preln_d1_seqx_r8_e9bd60'

def setup_inputs(seed: int=0):
    np.random.seed(seed)
    _w = jnp.asarray

    def _rec_inputs():
        import jax
        import jax.numpy as jnp
        _rk = jax.random.key(seed)
        x = -0.0003929 + 0.9999 * jax.random.normal(jax.random.fold_in(_rk, 1), (16, 56, 512), jnp.float32)
        _lenS = 56 - jax.random.randint(jax.random.fold_in(_rk, 7), (16,), 0, max(1, 56 // 4) + 1, jnp.int32)
        _lenS2 = 1500 - jax.random.randint(jax.random.fold_in(_rk, 8), (16,), 0, max(1, 1500 // 4) + 1, jnp.int32)
        _ctx_4096P = jax.random.normal(jax.random.fold_in(_rk, 11), (16, 16, 512), jnp.float32)
        _ctx_4096c = jax.random.dirichlet(jax.random.fold_in(_rk, 511), 0.3 * jnp.ones((16,), jnp.float32), (16, 1500))
        _ctx_4096t = jnp.einsum('bsk,bkd->bsd', _ctx_4096c, _ctx_4096P)
        _ctx_4096t = _ctx_4096t * jax.lax.rsqrt(jnp.mean(jnp.square(_ctx_4096t)) + 1e-12) * 0.953939
        ctx_4096 = 2.81802e-05 + 1.00001 * (_ctx_4096t + 0.3 * jax.random.normal(jax.random.fold_in(_rk, 611), (16, 1500, 512), jnp.float32))
        return (x, ctx_4096)
    x, ctx_4096 = _rec_inputs()

    def _L0_attn_setup():
        import jax, jax.numpy as jnp
        import numpy as np
        B, S, D = (2, 256, 512)
        NH, NKV = (32, 8)
        HD = D // NH
        NREP = NH // NKV
        SCALE = HD ** (-0.5)
        key = jax.random.key(seed)
        kx, kq, kk, kv, ko = jax.random.split(key, 5)
        s = 0.02
        return {'x': jax.random.normal(kx, (B, S, D), dtype=jnp.float32), 'wq': jax.random.normal(kq, (D, NH * HD), dtype=jnp.float32) * s, 'wk': jax.random.normal(kk, (D, NKV * HD), dtype=jnp.float32) * s, 'wv': jax.random.normal(kv, (D, NKV * HD), dtype=jnp.float32) * s, 'wo': jax.random.normal(ko, (NH * HD, D), dtype=jnp.float32) * s}
    _L0_attn_all = _L0_attn_setup()
    _L0_attn_in = {k: v for k, v in _L0_attn_all.items() if k in ('wq', 'wk', 'wv', 'wo')}
    del _L0_attn_all

    def _L0_xattn_setup():
        import jax, jax.numpy as jnp
        import numpy as np
        B, N, NKV = (2, 256, 256)
        E = 512
        H = 16
        HD = E // H
        LQ = E // 8
        LKV = E // 16
        key = jax.random.key(seed)
        ks = jax.random.split(key, 6)
        Q = jax.random.normal(ks[0], (B, N, E), dtype=jnp.float32)
        K = jax.random.normal(ks[1], (B, NKV, E), dtype=jnp.float32)
        Wq_d = jax.random.normal(ks[2], (E, LQ), dtype=jnp.float32) / np.sqrt(E)
        W_qk = jax.random.normal(ks[3], (LQ, H * LKV), dtype=jnp.float32) / np.sqrt(LQ)
        Wkv_d = jax.random.normal(ks[4], (E, LKV), dtype=jnp.float32) / np.sqrt(E)
        Wv_u = jax.random.normal(ks[5], (LKV, H * HD), dtype=jnp.float32) / np.sqrt(LKV)
        return {'Q': Q, 'K': K, 'Wq_d': Wq_d, 'W_qk': W_qk, 'Wkv_d': Wkv_d, 'Wv_u': Wv_u}
    _L0_xattn_all = _L0_xattn_setup()
    _L0_xattn_in = {k: v for k, v in _L0_xattn_all.items() if k in ('Wq_d', 'W_qk', 'Wkv_d', 'Wv_u')}
    del _L0_xattn_all

    def _L0_ffn_setup():
        import jax, jax.numpy as jnp
        import numpy as np
        B, T, D_IN, D_OUT = (8, 256, 512, 512)
        N_LORAS, RANK = (16, 32)
        SCALING = 1.0
        key = jax.random.key(seed)
        ks = jax.random.split(key, 8)
        std = 1.0 / D_IN ** 0.5
        x = jax.random.normal(ks[0], (B, T, D_IN), dtype=jnp.float32)
        idx = jax.random.randint(ks[1], (B,), 0, N_LORAS)
        gate = jax.nn.one_hot(idx, N_LORAS, dtype=jnp.float32)
        kernel = jax.random.normal(ks[2], (D_IN, D_OUT), dtype=jnp.float32) * std
        bias = jnp.zeros((D_OUT,), dtype=jnp.float32)
        lora_A = jax.random.normal(ks[3], (N_LORAS, RANK, D_IN), dtype=jnp.float32) * std
        lora_B = jax.random.normal(ks[4], (N_LORAS, D_OUT, RANK), dtype=jnp.float32) * 0.01
        lora_A_shared = jax.random.normal(ks[5], (RANK, D_IN), dtype=jnp.float32) * std
        lora_B_shared = jax.random.normal(ks[6], (D_OUT, RANK), dtype=jnp.float32) * 0.01
        return {'x': x, 'gate': gate, 'kernel': kernel, 'bias': bias, 'lora_A': lora_A, 'lora_B': lora_B, 'lora_A_shared': lora_A_shared, 'lora_B_shared': lora_B_shared}
    _L0_ffn_all = _L0_ffn_setup()
    _L0_ffn_in = {k: v for k, v in _L0_ffn_all.items() if k in ('gate', 'kernel', 'bias', 'lora_A', 'lora_B', 'lora_A_shared', 'lora_B_shared')}
    del _L0_ffn_all
    return {'x': x, 'ctx_4096': ctx_4096, 'L0_attn_wq': _L0_attn_in['wq'], 'L0_attn_wk': _L0_attn_in['wk'], 'L0_attn_wv': _L0_attn_in['wv'], 'L0_attn_wo': _L0_attn_in['wo'], 'L0_xattn_Wq_d': _L0_xattn_in['Wq_d'], 'L0_xattn_W_qk': _L0_xattn_in['W_qk'], 'L0_xattn_Wkv_d': _L0_xattn_in['Wkv_d'], 'L0_xattn_Wv_u': _L0_xattn_in['Wv_u'], 'L0_ffn_gate': _L0_ffn_in['gate'], 'L0_ffn_kernel': _L0_ffn_in['kernel'], 'L0_ffn_bias': _L0_ffn_in['bias'], 'L0_ffn_lora_A': _L0_ffn_in['lora_A'], 'L0_ffn_lora_B': _L0_ffn_in['lora_B'], 'L0_ffn_lora_A_shared': _L0_ffn_in['lora_A_shared'], 'L0_ffn_lora_B_shared': _L0_ffn_in['lora_B_shared']}

def reference(x, ctx_4096, L0_attn_wq, L0_attn_wk, L0_attn_wv, L0_attn_wo, L0_xattn_Wq_d, L0_xattn_W_qk, L0_xattn_Wkv_d, L0_xattn_Wv_u, L0_ffn_gate, L0_ffn_kernel, L0_ffn_bias, L0_ffn_lora_A, L0_ffn_lora_B, L0_ffn_lora_A_shared, L0_ffn_lora_B_shared):
    import jax
    import jax.numpy as jnp

    def _L0_attn_ref(x, wq, wk, wv, wo):
        import jax, jax.numpy as jnp
        import numpy as np
        B, S, D = (2, 256, 512)
        NH, NKV = (32, 8)
        HD = D // NH
        NREP = NH // NKV
        SCALE = HD ** (-0.5)
        b, s, _ = x.shape
        q = (x @ wq).reshape(b, s, NH, HD)
        k = (x @ wk).reshape(b, s, NKV, HD)
        v = (x @ wv).reshape(b, s, NKV, HD)
        k = jnp.repeat(k, NREP, axis=2)
        v = jnp.repeat(v, NREP, axis=2)
        scores = jnp.einsum('bihd,bjhd->bhij', q, k) * SCALE
        causal = jnp.tril(jnp.ones((s, s), dtype=bool))
        scores = jnp.where(causal, scores, jnp.finfo(scores.dtype).min)
        attn = jax.nn.softmax(scores, axis=-1)
        out = jnp.einsum('bhij,bjhd->bihd', attn, v)
        out = out.reshape(b, s, NH * HD)
        return out @ wo

    def _L0_xattn_ref(Q, K, Wq_d, W_qk, Wkv_d, Wv_u):
        import jax, jax.numpy as jnp
        import numpy as np
        B, N, NKV = (2, 256, 256)
        E = 512
        H = 16
        HD = E // H
        LQ = E // 8
        LKV = E // 16
        b, n, _ = Q.shape
        nkv = K.shape[1]
        C_q = Q @ Wq_d
        C_kv = K @ Wkv_d
        CqWqk = (C_q @ W_qk).reshape(b, n, H, LKV)
        scores = jnp.einsum('bnhl,bkl->bhnk', CqWqk, C_kv) / jnp.sqrt(jnp.asarray(LKV, dtype=Q.dtype))
        attn = jax.nn.softmax(scores, axis=-1)
        V_up = (C_kv @ Wv_u).reshape(b, nkv, H, HD)
        out = jnp.einsum('bhnk,bkhd->bnhd', attn, V_up)
        return out.reshape(b, n, H * HD)

    def _L0_ffn_ref(x, gate, kernel, bias, lora_A, lora_B, lora_A_shared, lora_B_shared):
        import jax, jax.numpy as jnp
        import numpy as np
        B, T, D_IN, D_OUT = (8, 256, 512, 512)
        N_LORAS, RANK = (16, 32)
        SCALING = 1.0
        base_out = jnp.matmul(x, kernel) + bias
        b = gate.shape[0]
        x_flat = x.reshape(b, -1, x.shape[-1])
        A_eff = jnp.einsum('bn,nri->bri', gate, lora_A)
        B_eff = jnp.einsum('bn,nor->bor', gate, lora_B)
        Ax = jnp.einsum('bri,bti->btr', A_eff, x_flat)
        delta_flat = jnp.einsum('bor,btr->bto', B_eff, Ax)
        Ax_s = jnp.einsum('ri,bti->btr', lora_A_shared, x_flat)
        delta_flat = delta_flat + jnp.einsum('or,btr->bto', lora_B_shared, Ax_s)
        delta = delta_flat.reshape(x.shape[:-1] + (kernel.shape[-1],))
        return base_out + (SCALING * delta).astype(base_out.dtype)
    x = x + _L0_attn_ref(_layernorm(x, axis=-1), L0_attn_wq, L0_attn_wk, L0_attn_wv, L0_attn_wo)
    x = x + _L0_xattn_ref(_layernorm(x, axis=-1), ctx_4096, L0_xattn_Wq_d, L0_xattn_W_qk, L0_xattn_Wkv_d, L0_xattn_Wv_u)
    x = x + _L0_ffn_ref(_layernorm(x, axis=-1), L0_ffn_gate, L0_ffn_kernel, L0_ffn_bias, L0_ffn_lora_A, L0_ffn_lora_B, L0_ffn_lora_A_shared, L0_ffn_lora_B_shared)
    return x

_drawn_inputs = setup_inputs


def setup_inputs(seed=0):
    import zlib

    import numpy as np

    out = dict(_drawn_inputs(seed))
    spreads = {'L0_ffn_bias': (0.0, 0.1)}
    factors = {'L0_attn_wq': 6.385, 'L0_attn_wk': 6.392}
    for name, (base, spread) in spreads.items():
        noise = np.random.default_rng([zlib.crc32(name.encode()), seed]).standard_normal(out[name].shape)
        drawn = base * np.exp(spread * noise) if base else spread * noise
        out[name] = jnp.asarray(drawn.astype(out[name].dtype))
    for name, factor in factors.items():
        out[name] = (out[name] * factor).astype(out[name].dtype)
    return out
```

```python
from contextlib import ExitStack

import concourse.bass as bass
from concourse import mybir

F32 = mybir.dt.float32
F32R = mybir.dt.float32r
ALU = mybir.AluOpType
ACT = mybir.ActivationFunctionType
AX = mybir.AxisListType

B, S, D = 16, 56, 512
PAIRS = B // 2
SLOT = 64
CH = D // 128
G, R, HD = 8, 4, 16
H, L = 16, 32
LQ = D // 8
NK = 1500
KT = NK // 4
KC = 125
KG = KT // KC
HN = H * S
HALF = HN // 2
ROWT = HN // 128
KP = NK // 3
PIECES = ROWT * 3
RANK, NL = 32, 16
EPS = 1e-5
NEG = -1e30
PR = 8
STB = 3
GROUPS = 2 * KG
ADDS = 4 * KG - 1
M_AT = [6, 5, 5, 5, 0, 0]
LOOP_BODIES = 2
FIRST_LOOPED, LAST_LOOPED = 1, 6
IDENT_MADE, MASKS_MADE, PADS_MADE, ALL_MADE = 2, 6, 12, 13
SEVENTH = [sum(M_AT[:g]) for g in range(GROUPS + 1)]

STEPS = [
    [],
    [("T1", "n"), ("A", "a")],
    [("KV", "n"), ("Q1", "n"), ("CT", "a")],
    [("S0", "n"), ("S1", "n"), ("S2", "n"), ("S3", "n")],
    [("MT", "m")],
    [("P0", "n"), ("P1", "n"), ("P2", "n"), ("P3", "n")],
    [("A", "b"), ("O1", "n"), ("XC", "f")],
    [("Y", "f"), ("W1", "n"), ("CT", "b")],
    [("DN", "f")],
    [("YT", "f"), ("T2", "n"), ("CQ", "n")],
    [("MT", "o"), ("T3", "f"), ("H0", "n"), ("H1", "n")],
    [("F1", "f"), ("F2", "f"), ("H2", "n"), ("H3", "n")],
]
BANK = {"T1": 0, "A": 1, "KV": 0, "Q1": 1, "CT": 0, "S0": 0, "S1": 1, "S2": 0, "S3": 1, "MT": 1,
        "P0": 0, "P1": 1, "P2": 0, "P3": 1, "O1": 0, "Y": 1, "W1": 0, "DN": 1, "YT": 0, "T2": 1,
        "CQ": 0, "T3": 0, "H0": 1, "H1": 0, "F1": 0, "F2": 1, "H2": 0, "H3": 1}


def steps_of(i, g):
    for name, w in STEPS[g]:
        n = {"n": i + 1, "f": i - 1, "a": 2 * i + 1, "b": 2 * i + 2, "m": 2 * i, "o": 2 * i + 1}[w]
        if 0 <= n < (PAIRS if w in "nf" else B):
            yield name, n


def decoder_layer(nc, x, ctx_t, wq, wk, wv, wo, wq_d, w_qk, wkv_d, wv_u, gate_t, kern, bias,
                  lora_a, lora_b, lora_as, lora_bs, out):
    with ExitStack() as stack:
        rates = {}

        def sb(name, shape, dt=F32):
            return stack.enter_context(nc.sbuf_tensor(name, shape, dt))

        def bank(name):
            return stack.enter_context(nc.psum_tensor(name, [128, 512], F32))

        def sem(name, per_pair):
            s = stack.enter_context(nc.semaphore(name))
            rates[s.name] = per_pair * LOOP_BODIES
            return s

        ctx_sb = sb("ctx_sb", [128, 2, CH, NK])
        wq_sb = sb("wq_sb", [128, CH, D])
        wk_sb = sb("wk_sb", [128, CH, 128])
        wv_sb = sb("wv_sb", [128, CH, 128])
        wo_sb = sb("wo_sb", [128, R, D])
        wqd_sb = sb("wqd_sb", [128, CH, LQ])
        wkv_sb = sb("wkv_sb", [128, CH, L])
        wqk_sb = sb("wqk_sb", [96, H, 3, L])
        wvu_sb = sb("wvu_sb", [128, D])
        kern_sb = sb("kern_sb", [128, CH, D])
        a_sb = sb("a_sb", [128, CH, 2 * RANK])
        b_sb = sb("b_sb", [96, D])
        c_st = sb("c_st", [98, 4, NK], F32R)
        c_nat = sb("c_nat", [KC, 4, KG, 128])
        q_st = sb("q_st", [98, 2, 2, HN], F32R)
        p_ring = sb("p_ring", [KC, PR, HALF])
        acc = sb("acc", [KC, 2, 2, HN])
        ox = sb("ox", [128, H, 2, S])
        p1 = sb("p1", [128, R * G, SLOT])
        p1t = sb("p1t", [128, G // 2, R, 128])
        x_sb = sb("x_sb", [128, 2, D])
        x2_sb = sb("x2_sb", [128, 2, D])
        xn = sb("xn", [128, D])
        x3 = sb("x3", [128, D])
        x3n = sb("x3n", [128, D])
        xnt = sb("xnt", [128, CH, 128])
        qt = sb("qt", [128, R, 128])
        khat = sb("khat", [128, 2, G, S])
        vhat = sb("vhat", [128, 2, G // 2, 2 * HD])
        cqt = sb("cqt", [96, 128])
        ct_f = sb("ct_f", [128, KT])
        ct_hl = sb("ct_hl", [128, 2, KT], F32R)
        mx_p = sb("mx_p", [128, PIECES])
        nm = sb("nm", [128, ROWT])
        nm_hl = sb("nm_hl", [128, 2, ROWT], F32R)
        m_t = sb("m_t", [2 * ROWT, 128])
        y_u = sb("y_u", [128, H // 4 * 2 * S])
        r_den = sb("r_den", [128, H // 4 * 2 * S])
        y_t = sb("y_t", [128, H // 4, 128])
        ax_t = sb("ax_t", [96, 128])
        sm = sb("sm", [128, 3, R * G])
        stats = sb("stats", [128, 3, 7])
        mv = sb("mv", [128, 3, 2])
        rstd = sb("rstd", [128, 3, 2])
        ident = sb("ident", [128, 128])
        ones = sb("ones", [128, 32])
        gmask = sb("gmask", [128, G])
        e8 = sb("e8", [128, 8])
        cmask = sb("cmask", [128, S])
        minus_half = sb("minus_half", [128, 1])
        eps_col = sb("eps_col", [128, 1])
        g8 = sb("g8", [128, PAIRS])
        gkron = sb("gkron", [128, PAIRS, 8])
        spare = ctx_sb[:, 1, :, :].rearrange("p c k -> p (c k)")
        lora_raw = [spare[:, 0:2048], spare[:, 2048:4096]]
        lora_eff = [p_ring[0:64, :, :].rearrange("p a b -> p (a b)"),
                    acc[0:64, :, :, :].rearrange("p a b c -> p (a b c)")]

        st_ps = [bank(f"st_ps{n}") for n in range(STB)]
        mx_ps = [bank(f"mx_ps{n}") for n in range(2)]
        pv_ps = bank("pv_ps")
        mi_ps = [bank(f"mi_ps{n}") for n in range(2)]

        a_eff = nc.dram_tensor("a_eff", [PAIRS, D, RANK], F32).ap()
        b_eff = nc.dram_tensor("b_eff", [PAIRS, RANK, D], F32).ap()

        x_in = [sem(f"x_in{n}", 16) for n in range(2)]
        ctx_in = [sem(f"ctx_in{n}", 16) for n in range(2)]
        ab_in = sem("ab_in", 32)
        for s in x_in + ctx_in:
            rates[s.name] = 32
        w_attn = sem("w_attn", 0)
        w_cross = sem("w_cross", 0)
        w_ffn = sem("w_ffn", 0)
        raw_in = sem("raw_in", 0)
        eff_out = sem("eff_out", 0)
        cst_in = [sem(f"cst_in{n}", 0) for n in range(4)]
        for s in cst_in:
            rates[s.name] = 16 * 12
        m_in = [sem(f"m_in{n}", 32) for n in range(2)]
        y_out = sem("y_out", 32)
        pool_c = sem("pool_c", 0)
        dve_c = sem("dve_c", 0)
        lora_ps = sem("lora_ps", 0)
        lora_sb = sem("lora_sb", 0)
        ln = [sem("ln0", 3), sem("ln1", 4), sem("ln2", 4)]
        ln_eps = [sem(f"ln_eps{n}", 1) for n in range(3)]
        x3_base = sem("x3_base", 1)
        ln_pow = [sem(f"ln_pow{n}", 1) for n in range(3)]
        st_done = sem("st_done", 48)
        exp_done = sem("exp_done", 48)
        pv_done = sem("pv_done", 12)
        ox_sb = sem("ox_sb", 4)
        acc_done = sem("acc_done", 4 * ADDS)
        mx_done = sem("mx_done", 2 * PIECES)
        red_done = sem("red_done", 2 * PIECES)
        nm_step = sem("nm_step", 2 * 3)
        ps = {}
        for name in BANK:
            ps[name] = sem("ps_" + name, 2 if name in ("A", "CT", "MT") else 1)
        t1_sb = sem("t1_sb", 1)
        k_sb = sem("k_sb", 2)
        v_sb = sem("v_sb", 2)
        q1_sb = sem("q1_sb", 1)
        s1_sb = sem("s1_sb", 4)
        soft = sem("soft", 2)
        soft_e = sem("soft_e", 1)
        soft_n = sem("soft_n", 3)
        pt_sb = sem("pt_sb", 4)
        o1_sb = sem("o1_sb", 1)
        t2_sb = sem("t2_sb", 1)
        cq_sb = sem("cq_sb", 1)
        qh_hi = sem("qh_hi", 4)
        qh_lo = sem("qh_lo", 4)
        a_f = sem("a_f", 2)
        a_hi = sem("a_hi", 2)
        a_lo = sem("a_lo", 2)
        ct_sb = sem("ct_sb", 2)
        mt_sb = sem("mt_sb", 2)
        yu_sb = sem("yu_sb", 1)
        yn_step = sem("yn_step", 2)
        t3_sb = sem("t3_sb", 1)
        f1_sb = sem("f1_sb", 1)
        f2_sb = sem("f2_sb", 1)

        def lora_bank(q):
            return [*st_ps, *mx_ps, pv_ps][q % 6]

        block = stack.enter_context(nc.Block())

        def counter(at):
            def due(s, count):
                assert count > 0
                return count if at[0] is None else at[0] * rates[s.name] + count
            return due

        def run_bodies(eng, at, body):
            body(0)
            with eng.Fori(0, (LAST_LOOPED - FIRST_LOOPED + 1) // LOOP_BODIES) as rnd:
                at[0] = rnd
                for i in range(FIRST_LOOPED, FIRST_LOOPED + LOOP_BODIES):
                    body(i)
                at[0] = None
            for i in range(LAST_LOOPED + 1, PAIRS + 1):
                body(i)

        @block.sync
        def _(sp):
            at = [None]
            due = counter(at)
            dma = sp.dma_start

            def pair_index(n):
                return n if at[0] is None else at[0] * LOOP_BODIES + n

            def batch_index(b):
                return b if at[0] is None else at[0] * (2 * LOOP_BODIES) + b

            def load_x(n):
                if n >= 2:
                    sp.wait_ge(ln[1], due(ln[1], 4 * (n - 2) + 1))
                for h in range(2):
                    dma(x_sb[h * SLOT:h * SLOT + S, n % 2, :], x[pair_index(n), h]).then_inc(x_in[n % 2], 16)

            def load_ctx(b):
                if b >= 2:
                    sp.wait_ge(ps["A"], due(ps["A"], b - 1))
                dma(ctx_sb[:, b % 2, :, :],
                    ctx_t[batch_index(b)].rearrange("(p c) k -> p c k", c=CH)).then_inc(ctx_in[b % 2], 16)

            def load_ab(n):
                dma(a_sb[:, :, 0:RANK],
                    a_eff[pair_index(n)].rearrange("(c p) r -> p c r", p=128)).then_inc(ab_in, 16)
                dma(b_sb[0:RANK, :], b_eff[pair_index(n)]).then_inc(ab_in, 16)

            def spread_ct(b):
                for part, dst in ((0, 0), (1, L), (0, 2 * L)):
                    if dst == 0:
                        sp.wait_ge(a_hi, due(a_hi, b + 1))
                    if dst == L:
                        sp.wait_ge(a_lo, due(a_lo, b + 1))
                    for t in range(4):
                        dma(c_st[dst:dst + L, b % 4, t * KT:(t + 1) * KT].bitcast(F32),
                            ct_hl[t * L:(t + 1) * L, part, :].bitcast(F32)).then_inc(cst_in[b % 4], 16)

            def spread_m(b):
                sp.wait_ge(mt_sb, due(mt_sb, b + 1))
                for part in range(2):
                    dma(q_st[96 + part:97 + part, b // 2 % 2, b % 2, :].bitcast(F32)
                        .rearrange("a (j p) -> a j p", p=128),
                        m_t[part * ROWT:(part + 1) * ROWT, :]).then_inc(m_in[b % 2], 16)

            def store_y(n):
                sp.wait_ge(f2_sb, due(f2_sb, n + 1))
                for h in range(2):
                    dma(out[pair_index(n), h], x3n[h * SLOT:h * SLOT + S, :]).then_inc(y_out, 16)

            sp.wait_ge(dve_c, due(dve_c, 1))
            load_x(0)
            for c in range(2):
                dma(wq_sb[:, 2 * c:2 * c + 2, :], wq[c * 256:(c + 1) * 256, :].rearrange("(c p) n -> p c n", p=128))\
                    .then_inc(w_attn, 16)
            dma(wk_sb[:, :, :], wk.rearrange("(c p) n -> p c n", p=128)).then_inc(w_attn, 16)
            dma(wv_sb[:, :, :], wv.rearrange("(c p) n -> p c n", p=128)).then_inc(w_attn, 16)
            dma(wkv_sb[:, :, :], wkv_d.rearrange("(p c) n -> p c n", c=CH)).then_inc(w_cross, 16)
            load_ctx(0)
            dma(wo_sb[:, :, :], wo.rearrange("(r p) n -> p r n", p=128)).then_inc(w_attn, 16)
            dma(wqd_sb[:, :, :], wq_d.rearrange("(c p) n -> p c n", p=128)).then_inc(w_cross, 16)
            for k in range(3):
                dma(wqk_sb[0:LQ, :, k, :], w_qk.rearrange("p (h l) -> p h l", l=L)).then_inc(w_cross, 16)
            for t in range(4):
                dma(wvu_sb[t * L:(t + 1) * L, :], wv_u).then_inc(w_cross, 16)
            for k in range(2):
                dma(lora_raw[k], (lora_a, lora_b)[k].rearrange("n (e f) r -> (n e) (f r)", e=8)).then_inc(raw_in, 16)
            dma(g8[:, :], gate_t).then_inc(raw_in, 16)
            spread_ct(0)
            sp.wait_ge(lora_ps, due(lora_ps, 8))
            load_ctx(1)
            dma(kern_sb[:, :, :], kern.rearrange("(c p) n -> p c n", p=128)).then_inc(w_ffn, 16)
            sp.wait_ge(pool_c, due(pool_c, PADS_MADE))
            dma(a_sb[:, :, RANK:2 * RANK], lora_as.rearrange("(c p) r -> p c r", p=128)).then_inc(w_ffn, 16)
            dma(b_sb[RANK:2 * RANK, :], lora_bs).then_inc(w_ffn, 16)
            dma(b_sb[2 * RANK:2 * RANK + 1, :], bias).then_inc(y_out, 16)
            sp.wait_ge(eff_out, due(eff_out, 32))

            def body(i):
                if 2 * i + 2 < B:
                    load_x(i + 1)
                    load_ctx(2 * i + 2)
                for g in range(2 * GROUPS):
                    for name, n in steps_of(i, g):
                        if name == "A":
                            spread_ct(n)
                            if n % 2 and n + 2 < B:
                                load_ctx(n + 2)
                        elif name == "MT":
                            spread_m(n)
                        elif name == "Y":
                            load_ab(n)
                        elif name == "F2":
                            store_y(n)

            run_bodies(sp, at, body)
            sp.wait_ge(y_out, due(y_out, 32 * PAIRS + 16))

        @block.tensor
        def _(pe):
            at = [None]
            due = counter(at)
            mm = pe.matmul

            def four_transposes(bank_, src):
                for c in range(4):
                    last = pe.transpose(bank_[:, c * 128:(c + 1) * 128], src[:, c * 128:(c + 1) * 128], ident[:, :])
                return last

            def step(name, n):
                if name == "XC":
                    return
                o = mi_ps[BANK[name]]
                slot = n % 2
                if name == "T1":
                    if n:
                        pe.wait_ge(qh_lo, due(qh_lo, 4 * n - 1))
                    pe.wait_ge(ln[0], due(ln[0], 3 * n + 3))
                    last = four_transposes(o, xn)
                elif name == "KV":
                    pe.wait_ge(t1_sb, due(t1_sb, n + 1))
                    for c in range(CH):
                        mm(o[:, 0:128], wk_sb[:, c, :], xnt[:, c, :], start=(c == 0), stop=(c == CH - 1))
                    for b in range(2):
                        for c in range(CH):
                            for h in range(2):
                                last = mm(o[h * 64:h * 64 + 64, 128 + b * 128:256 + b * 128],
                                          xnt[:, c, b * SLOT:(b + 1) * SLOT], wv_sb[:, c, :],
                                          start=(c == 0), stop=(c == CH - 1))
                elif name == "Q1":
                    if n:
                        pe.wait_ge(a_f, due(a_f, 2 * n))
                    for r in range(R):
                        for c in range(CH):
                            last = mm(o[:, r * 128:(r + 1) * 128], wq_sb[:, c, r * 128:(r + 1) * 128],
                                      xnt[:, c, :], start=(c == 0), stop=(c == CH - 1))
                elif name in ("S0", "S1", "S2", "S3"):
                    r = int(name[1])
                    if r == 0 and n:
                        pe.wait_ge(ct_sb, due(ct_sb, 2 * n))
                    if r >= 2:
                        pe.wait_ge(s1_sb, due(s1_sb, 4 * n + r - 1))
                    if r == 0:
                        pe.wait_ge(q1_sb, due(q1_sb, n + 1))
                        pe.wait_ge(k_sb, due(k_sb, 2 * n + 2))
                    for b in range(2):
                        last = mm(o[b * SLOT:(b + 1) * SLOT, 0:G * S], qt[:, r, b * SLOT:(b + 1) * SLOT],
                                  khat[:, b, :, :].rearrange("p g k -> p (g k)"), start=True, stop=True)
                elif name in ("P0", "P1", "P2", "P3"):
                    r = int(name[1])
                    if r == 0:
                        pe.wait_ge(soft_n, due(soft_n, 3 * n + 3))
                    if r == 1 and n:
                        pe.wait_ge(mt_sb, due(mt_sb, 2 * n - 1))
                    if r >= 2:
                        pe.wait_ge(pt_sb, due(pt_sb, 4 * n + r - 1))
                    last = four_transposes(o, p1[:, r * G:(r + 1) * G, :].rearrange("p g k -> p (g k)"))
                elif name == "O1":
                    pe.wait_ge(pt_sb, due(pt_sb, 4 * n + 4))
                    pe.wait_ge(v_sb, due(v_sb, 2 * n + 2))
                    for b in range(2):
                        for g in range(G // 2):
                            last = mm(o[g * 32:(g + 1) * 32, b * 256:(b + 1) * 256], vhat[:, b, g, :],
                                      p1t[:, g, :, b * SLOT:(b + 1) * SLOT], start=True, stop=True)
                elif name == "W1":
                    pe.wait_ge(o1_sb, due(o1_sb, n + 1))
                    for r in range(R):
                        last = mm(o[:, :], qt[:, r, :], wo_sb[:, r, :], start=(r == 0), stop=(r == R - 1))
                elif name == "T2":
                    if n >= 2:
                        pe.wait_ge(yn_step, due(yn_step, 2 * n - 3))
                    pe.wait_ge(ln[1], due(ln[1], 4 * n + 4))
                    last = four_transposes(o, xn)
                elif name == "CQ":
                    if n >= 2:
                        pe.wait_ge(ln[2], due(ln[2], 4 * n - 7))
                    if n == 1:
                        pe.wait_ge(ct_sb, due(ct_sb, 3))
                    pe.wait_ge(t2_sb, due(t2_sb, n + 1))
                    for c in range(CH):
                        last = mm(o[0:LQ, 0:128], wqd_sb[:, c, :], xnt[:, c, :], start=(c == 0), stop=(c == CH - 1))
                elif name in ("H0", "H1", "H2", "H3"):
                    k = int(name[1])
                    if k == 0:
                        pe.wait_ge(cq_sb, due(cq_sb, n + 1))
                    if k == 0 and n:
                        pe.wait_ge(mt_sb, due(mt_sb, 2 * n))
                    if k == 1 and n >= 2:
                        pe.wait_ge(t3_sb, due(t3_sb, n - 1))
                    if k == 2 and n < 2:
                        pe.wait_ge(qh_lo, due(qh_lo, 4 * n + 2))
                    if k == 3 and n < 2:
                        pe.wait_ge(qh_lo, due(qh_lo, 4 * n + 1))
                    if k == 3 and n >= 2:
                        pe.wait_ge(f2_sb, due(f2_sb, n - 1))
                    for h in range(4):
                        head = 4 * k + h
                        last = mm(o[0:96, h * 2 * S:(h + 1) * 2 * S], wqk_sb[:, head, :, :].rearrange("p k l -> p (k l)"),
                                  cqt[:, :].rearrange("p (b s) -> p b s", b=2)[:, :, 0:S], start=True, stop=True)
                elif name == "A":
                    if n % 2:
                        pe.wait_ge(qh_lo, due(qh_lo, 2 * n + 2))
                    elif n:
                        pe.wait_ge(pt_sb, due(pt_sb, 2 * n + 4))
                    pe.wait_ge(ctx_in[slot], due(ctx_in[slot], 16 * (n // 2 + 1)))
                    for c in range(CH):
                        for t in range(4):
                            last = mm(o[t * L:(t + 1) * L, 0:KT], wkv_sb[:, c, :],
                                      ctx_sb[:, slot, c, t * KT:(t + 1) * KT], start=(c == 0), stop=(c == CH - 1))
                elif name == "CT":
                    if n % 2 and n + 1 < B:
                        pe.wait_ge(v_sb, due(v_sb, n + 3))
                    if n % 2 == 0 and n:
                        pe.wait_ge(ln[1], due(ln[1], 2 * n + 1))
                    pe.wait_ge(a_f, due(a_f, n + 1))
                    for k in range(KG):
                        last = pe.transpose(o[0:KC, k * 128:(k + 1) * 128], ct_f[:, k * KC:(k + 1) * KC], ident[:, :])
                elif name == "MT":
                    if n % 2 == 0 and n + 2 < B:
                        pe.wait_ge(s1_sb, due(s1_sb, 2 * n + 8))
                    pe.wait_ge(nm_step, due(nm_step, 3 * n + 3))
                    last = pe.transpose(o[0:2 * ROWT, 0:128],
                                        nm_hl[:, :, :].rearrange("p a j -> p (a j)").bitcast(F32), ident[:, :])
                elif name == "Y":
                    if 2 * n + 4 < B:
                        pe.wait_ge(a_f, due(a_f, 2 * n + 5))
                    if n == PAIRS - 2:
                        pe.wait_ge(mt_sb, due(mt_sb, B - 1))
                    if n == PAIRS - 1:
                        pe.wait_ge(f2_sb, due(f2_sb, PAIRS - 1))
                    pe.wait_ge(ox_sb, due(ox_sb, 4 * n + 4))
                    for h in range(H):
                        t, q = h % 4, h // 4
                        last = mm(o[t * 32:(t + 1) * 32, q * 2 * S:(q + 1) * 2 * S], wvu_sb[:, h * L:(h + 1) * L],
                                  ox[:, h, :, :].rearrange("p b s -> p (b s)"), start=True, stop=True)
                elif name == "DN":
                    pe.wait_ge(yu_sb, due(yu_sb, n + 1))
                    pe.wait_ge(acc_done, due(acc_done, 4 * ADDS * (n + 1)))
                    for h in range(H):
                        t, q = h % 4, h // 4
                        last = mm(o[t * 32:(t + 1) * 32, q * 2 * S:(q + 1) * 2 * S], ones[0:KC, :],
                                  acc[:, slot, :, h * S:(h + 1) * S], start=True, stop=True)
                elif name == "YT":
                    pe.wait_ge(ct_sb, due(ct_sb, min(2 * n + 5, B)))
                    pe.wait_ge(yn_step, due(yn_step, 2 * n + 2))
                    last = four_transposes(o, y_t[:, :, :].rearrange("p q s -> p (q s)"))
                elif name == "T3":
                    if n + 2 < PAIRS:
                        pe.wait_ge(cq_sb, due(cq_sb, n + 3))
                    pe.wait_ge(ln[2], due(ln[2], 4 * n + 4))
                    last = four_transposes(o, x3n)
                elif name == "F1":
                    if n + 2 < PAIRS:
                        pe.wait_ge(qh_lo, due(qh_lo, 4 * n + 10))
                    pe.wait_ge(t3_sb, due(t3_sb, n + 1))
                    pe.wait_ge(ab_in, due(ab_in, 32 * (n + 1)))
                    for c in range(CH):
                        last = mm(o[0:2 * RANK, 0:128], a_sb[:, c, :], xnt[:, c, :],
                                  start=(c == 0), stop=(c == CH - 1))
                elif name == "F2":
                    if n == PAIRS - 2:
                        pe.wait_ge(mt_sb, due(mt_sb, B))
                    for c in range(CH):
                        mm(o[:, :], xnt[:, c, :], kern_sb[:, c, :], start=(c == 0), stop=False)
                    pe.wait_ge(f1_sb, due(f1_sb, n + 1))
                    last = mm(o[:, :], ax_t[:, :], b_sb[:, :], start=False, stop=True)
                last.then_inc(ps[name], 1)

            def scores(b, g, t):
                unit = b * 24 + g * 4 + t
                half, k = g // KG, g % KG
                if g == 0 and t == 0:
                    pe.wait_ge(m_in[b % 2], due(m_in[b % 2], 32 * (b // 2 + 1)))
                if unit >= STB:
                    pe.wait_ge(exp_done, due(exp_done, unit - STB + 1))
                mm(st_ps[unit % STB][0:KC, 0:HALF], c_st[:, b % 4, t * KT + k * KC:t * KT + (k + 1) * KC],
                   q_st[:, b // 2 % 2, b % 2, half * HALF:(half + 1) * HALF],
                   start=True, stop=True).then_inc(st_done, 1)

            def sums(b, g):
                half, k = g // KG, g % KG
                pe.wait_ge(exp_done, due(exp_done, b * 24 + g * 4 + 4))
                if g == 0:
                    pe.wait_ge(ct_sb, due(ct_sb, b + 1))
                if k == 0 and b * 2 + half:
                    pe.wait_ge(ox_sb, due(ox_sb, b * 2 + half))
                for t in range(4):
                    unit = b * 24 + g * 4 + t
                    last = mm(pv_ps[t * L:(t + 1) * L, 0:HALF], c_nat[:, b % 4, k, t * L:(t + 1) * L],
                              p_ring[:, unit % PR, :], start=(k == 0), stop=(k == KG - 1))
                last.then_inc(pv_done, 1)

            def maxima(b, p):
                j, k = p // 3, p % 3
                if p == 0:
                    pe.wait_ge(cst_in[b % 4], due(cst_in[b % 4], 16 * 12 * (b // 4 + 1)))
                if k == 0:
                    pe.wait_ge(qh_lo, due(qh_lo, 4 * (b // 2) + ((j + 1) * 128 - 1) // (4 * S) + 1))
                if b * PIECES + p >= 2:
                    pe.wait_ge(red_done, due(red_done, b * PIECES + p - 1))
                mm(mx_ps[(b * PIECES + p) % 2][:, 0:KP], q_st[0:96, b // 2 % 2, b % 2, j * 128:(j + 1) * 128],
                   c_st[0:96, b % 4, k * KP:(k + 1) * KP], start=True, stop=True).then_inc(mx_done, 1)

            def lora_factors():
                pe.wait_ge(raw_in, due(raw_in, 16 * 3))
                pe.wait_ge(dve_c, due(dve_c, 4))
                for q in range(8):
                    if q >= 6:
                        pe.wait_ge(lora_sb, due(lora_sb, q - 5))
                    mm(lora_bank(q)[0:64, :], gkron[:, :, :].rearrange("p i e -> p (i e)"),
                       lora_raw[q // 4][:, q % 4 * 512:(q % 4 + 1) * 512], start=True, stop=True)\
                        .then_inc(lora_ps, 1)

            pe.wait_ge(pool_c, due(pool_c, IDENT_MADE))
            step("T1", 0)
            pe.wait_ge(w_attn, due(w_attn, 16 * 5))
            step("KV", 0)
            step("Q1", 0)
            pe.wait_ge(w_cross, due(w_cross, 16 * 9))
            pe.wait_ge(dve_c, due(dve_c, 3))
            pe.wait_ge(pool_c, due(pool_c, PADS_MADE))
            pe.wait_ge(q1_sb, due(q1_sb, 1))
            step("A", 0)
            pe.wait_ge(v_sb, due(v_sb, 2))
            step("S0", 0)
            pe.wait_ge(a_f, due(a_f, 1))
            for name in ("S1", "S2", "S3"):
                step(name, 0)
            pe.wait_ge(s1_sb, due(s1_sb, 3))
            step("CT", 0)
            lora_factors()
            pe.wait_ge(ct_sb, due(ct_sb, 1))
            for name in ("P0", "P1", "P2", "P3", "O1", "W1", "T2", "CQ", "H0", "H1", "H2", "H3"):
                step(name, 0)
            pe.wait_ge(w_ffn, due(w_ffn, 16 * 3))
            pe.wait_ge(y_out, due(y_out, 16))
            pe.wait_ge(lora_sb, due(lora_sb, 8))
            pe.wait_ge(pool_c, due(pool_c, ALL_MADE))

            def body(i):
                for g in range(2 * GROUPS):
                    part, gg = g // GROUPS, g % GROUPS
                    bs, bm = 2 * i - 1 + part, 2 * i + part
                    todo = list(range(SEVENTH[gg], SEVENTH[gg + 1])) if bm < B else []
                    for t in range(4):
                        if 0 <= bs < B:
                            scores(bs, gg, t)
                        for p in todo[t * len(todo) // 4:(t + 1) * len(todo) // 4]:
                            maxima(bm, p)
                    bl, gl = (bs, gg - 1) if gg else (bs - 1, GROUPS - 1)
                    if 0 <= bl < B:
                        sums(bl, gl)
                    for name, n in steps_of(i, g):
                        step(name, n)

            run_bodies(pe, at, body)

        @block.scalar
        def _(act):
            at = [None]
            due = counter(at)

            def copy(dst, src, scale=1.0):
                return act.activation(dst, src, ACT.Copy, scale=scale)

            def step(name, n):
                if name == "XC":
                    act.wait_ge(ln[1], due(ln[1], 4 * n + 4))
                    if n + 2 >= PAIRS:
                        act.wait_ge(f2_sb, due(f2_sb, n))
                    copy(x3[:, :], x2_sb[:, n % 2, :]).then_inc(x3_base, 1)
                    return
                if name not in ("T1", "KV", "Q1", "P0", "P1", "P2", "P3", "S3", "O1", "T2", "CQ", "H0", "H1", "H2",
                                "H3", "A", "CT", "MT", "Y", "T3", "F1"):
                    return
                o = mi_ps[BANK[name]]
                if name == "S3":
                    act.wait_ge(soft, due(soft, 2 * n + 2))
                    act.activation(p1[:, :, 0:S], p1[:, :, 0:S], ACT.Exp).then_inc(soft_e, 1)
                    return
                act.wait_ge(ps[name], due(ps[name], n + 1))
                if name == "T1":
                    copy(xnt[:, :, :].rearrange("p c s -> p (c s)"), o[:, :]).then_inc(t1_sb, 1)
                elif name == "KV":
                    act.wait_ge(k_sb, due(k_sb, 2 * n + 2))
                    for h in range(2):
                        src = o[h * 64:(h + 1) * 64, 128:384].rearrange("p (b g e d) -> p b g e d", b=2, g=4, e=2)
                        copy(vhat[h * 64:(h + 1) * 64, :, :, h * HD:(h + 1) * HD], src[:, :, :, h, :])\
                            .then_inc(v_sb, 1)
                elif name == "Q1":
                    copy(qt[:, :, :].rearrange("p r s -> p (r s)"), o[:, :], scale=float(HD) ** -0.5)\
                        .then_inc(q1_sb, 1)
                elif name[0] == "P":
                    copy(p1t[:, :, int(name[1]), :], o[:, :].rearrange("p (g s) -> p g s", g=4)).then_inc(pt_sb, 1)
                elif name == "O1":
                    copy(qt[:, :, :].rearrange("p r (b s) -> p b r s", b=2),
                         o[:, :].rearrange("p (b r s) -> p b r s", b=2, r=R)).then_inc(o1_sb, 1)
                elif name == "T2":
                    copy(xnt[:, :, :].rearrange("p c s -> p (c s)"), o[:, :]).then_inc(t2_sb, 1)
                elif name == "CQ":
                    copy(cqt[0:LQ, :], o[0:LQ, 0:128]).then_inc(cq_sb, 1)
                elif name[0] == "H":
                    k = int(name[1])
                    if n >= 2:
                        act.wait_ge(st_done, due(st_done, 24 * (2 * n - 2)))
                    for b in range(2):
                        last = copy(q_st[0:96, n % 2, b, k * 4 * S:(k + 1) * 4 * S].rearrange("p (h s) -> p h s", h=4),
                                    o[0:96, 0:448].rearrange("p (h b s) -> p b h s", b=2, s=S)[:, b])
                    last.then_inc(qh_hi, 1)
                elif name == "A":
                    if n:
                        act.wait_ge(a_lo, due(a_lo, n))
                    copy(ct_f[:, :], o[:, 0:KT]).then_inc(a_f, 1)
                elif name == "CT":
                    copy(c_nat[:, n % 4, :, :].rearrange("p k l -> p (k l)"), o[0:KC, 0:KG * 128])\
                        .then_inc(ct_sb, 1)
                elif name == "MT":
                    if n:
                        act.wait_ge(m_in[(n - 1) % 2], due(m_in[(n - 1) % 2], 32 * ((n - 1) // 2 + 1)))
                    copy(m_t[:, :], o[0:2 * ROWT, 0:128]).then_inc(mt_sb, 1)
                elif name == "Y":
                    copy(y_u[:, :], o[:, 0:448]).then_inc(yu_sb, 1)
                elif name == "T3":
                    copy(xnt[:, :, :].rearrange("p c s -> p (c s)"), o[:, :]).then_inc(t3_sb, 1)
                elif name == "F1":
                    copy(ax_t[0:2 * RANK, :], o[0:2 * RANK, 0:128]).then_inc(f1_sb, 1)

            def exponentials(b, g):
                half = g // KG
                for t in range(4):
                    unit = b * 24 + g * 4 + t
                    act.wait_ge(st_done, due(st_done, unit + 1))
                    old = unit - PR
                    if old >= 0:
                        act.wait_ge(pv_done, due(pv_done, old // 4 + 1))
                        act.wait_ge(acc_done, due(acc_done, old // 12 * ADDS + max(old % 12, 1)))
                    act.activation(p_ring[:, unit % PR, :], st_ps[unit % STB][0:KC, 0:HALF], ACT.Exp,
                                   scale=float(L) ** -0.5).then_inc(exp_done, 1)

            def out_of_sums(b, half):
                act.wait_ge(pv_done, due(pv_done, b * 6 + half * KG + KG))
                if b % 2 == 0 and half == 0 and b:
                    act.wait_ge(ps["Y"], due(ps["Y"], b // 2))
                copy(ox[:, half * 8:half * 8 + 8, b % 2, :],
                     pv_ps[:, 0:HALF].rearrange("p (h s) -> p h s", h=8)).then_inc(ox_sb, 1)

            act.wait_ge(dve_c, due(dve_c, 2))
            for name in ("T1", "KV", "Q1", "A", "S3", "CT"):
                step(name, 0)
            for q in range(8):
                act.wait_ge(lora_ps, due(lora_ps, q + 1))
                copy(lora_eff[q // 4][:, q % 4 * 512:(q % 4 + 1) * 512], lora_bank(q)[0:64, :]).then_inc(lora_sb, 1)
            act.wait_ge(lora_sb, due(lora_sb, 8))
            for k, dst in enumerate((a_eff, b_eff)):
                act.dma_start(dst.rearrange("i (e f) r -> (i e) (f r)", e=8), lora_eff[k][:, 0:2048])\
                    .then_inc(eff_out, 16)
            for name in ("P0", "P1", "P2", "P3", "O1", "T2", "CQ", "H0", "H1", "H2", "H3"):
                step(name, 0)
            act.wait_ge(eff_out, due(eff_out, 32))

            def body(i):
                for g in range(2 * GROUPS):
                    part, gg = g // GROUPS, g % GROUPS
                    bs = 2 * i - 1 + part
                    if 0 <= bs < B:
                        exponentials(bs, gg)
                    bl, gl = (bs, gg - 1) if gg else (bs - 1, GROUPS - 1)
                    if 0 <= bl < B and gl % KG == KG - 1:
                        out_of_sums(bl, gl // KG)
                    for name, n in steps_of(i, g):
                        step(name, n)

            run_bodies(act, at, body)

        @block.vector
        def _(ve):
            at = [None]
            due = counter(at)

            def layer_norm(which, n, src, dst):
                s = ln[which]
                k = 3 * n if which == 0 else 4 * n + 1
                ve.bn_stats(stats[:, which, 0:6], src).then_inc(s, 1)
                ve.wait_ge(s, due(s, k + 1))
                ve.tensor_copy(stats[:, which, 6:7], eps_col[:, :])
                ve.bn_aggr(mv[:, which, :], stats[:, which, 0:6]).then_inc(s, 1)
                ve.wait_ge(ln_pow[which], due(ln_pow[which], n + 1))
                ve.tensor_scalar(dst, src, mv[:, which, 0:1], rstd[:, which, 1:2], ALU.subtract, ALU.mult)\
                    .then_inc(s, 1)

            def step(name, n):
                if name not in BANK:
                    return
                o = mi_ps[BANK[name]]
                slot = n % 2
                if name in ("KV", "W1", "H0", "H1", "H2", "H3", "DN", "YT", "F2") or name in ("S0", "S1", "S2", "S3"):
                    ve.wait_ge(ps[name], due(ps[name], n + 1))
                if name == "KV":
                    for b in range(2):
                        k = o[:, b * SLOT:b * SLOT + S].unsqueeze(1).to_broadcast([128, G, S])
                        ve.tensor_tensor(khat[:, b, :, :], k, gmask[:, :].unsqueeze(2).to_broadcast([128, G, S]),
                                         ALU.mult).then_inc(k_sb, 1)
                elif name in ("S0", "S1", "S2", "S3"):
                    r = int(name[1])
                    ve.tensor_tensor(p1[:, r * G:(r + 1) * G, 0:S], o[:, 0:G * S].rearrange("p (g k) -> p g k", g=G),
                                     cmask[:, :].unsqueeze(1).to_broadcast([128, G, S]), ALU.add)\
                        .then_inc(s1_sb, 1)
                    if r == 3:
                        softmax(n)
                elif name == "W1":
                    if n >= 2:
                        ve.wait_ge(x3_base, due(x3_base, n - 1))
                    ve.tensor_tensor(x2_sb[:, slot, :], o[:, :], x_sb[:, slot, :], ALU.add).then_inc(ln[1], 1)
                    ve.wait_ge(ln[1], due(ln[1], 4 * n + 1))
                    layer_norm(1, n, x2_sb[:, slot, :], xn[:, :])
                elif name[0] == "H":
                    k = int(name[1])
                    ve.wait_ge(qh_hi, due(qh_hi, 4 * n + k + 1))
                    for b in range(2):
                        q = q_st[64:96, slot, b, k * 4 * S:(k + 1) * 4 * S].rearrange("p (h s) -> p h s", h=4)
                        last = ve.tensor_tensor(q, o[64:96, 0:448].rearrange("p (h b s) -> p b h s", b=2, s=S)[:, b],
                                                q.bitcast(F32), ALU.subtract)
                    last.then_inc(qh_lo, 1)
                elif name == "A":
                    if n:
                        ve.wait_ge(cst_in[(n - 1) % 4], due(cst_in[(n - 1) % 4], 16 * 12 * ((n - 1) // 4 + 1)))
                    ve.wait_ge(a_f, due(a_f, n + 1))
                    ve.tensor_copy(ct_hl[:, 0, :], ct_f[:, :]).then_inc(a_hi, 1)
                    ve.wait_ge(a_hi, due(a_hi, n + 1))
                    ve.tensor_tensor(ct_hl[:, 1, :], ct_f[:, :], ct_hl[:, 0, :].bitcast(F32), ALU.subtract)\
                        .then_inc(a_lo, 1)
                elif name == "DN":
                    ve.reciprocal(r_den[:, :], o[:, 0:448]).then_inc(yn_step, 1)
                    ve.wait_ge(yn_step, due(yn_step, 2 * n + 1))
                    ve.wait_ge(yu_sb, due(yu_sb, n + 1))
                    ve.tensor_tensor(y_t[:, :, :].rearrange("p q (b s) -> p q b s", b=2)[:, :, :, 0:S],
                                     y_u[:, :].rearrange("p (q b s) -> p q b s", q=4, b=2),
                                     r_den[:, :].rearrange("p (q b s) -> p q b s", q=4, b=2), ALU.mult)\
                        .then_inc(yn_step, 1)
                elif name == "YT":
                    ve.wait_ge(y_out, due(y_out, 32 * n + 16))
                    ve.wait_ge(x3_base, due(x3_base, n + 1))
                    ve.tensor_tensor(x3[:, :], o[:, :], x3[:, :], ALU.add).then_inc(ln[2], 1)
                    ve.wait_ge(ln[2], due(ln[2], 4 * n + 1))
                    layer_norm(2, n, x3[:, :], x3n[:, :])
                elif name == "F2":
                    ve.tensor_tensor(x3n[:, :], o[:, :], x3[:, :], ALU.add).then_inc(f2_sb, 1)

            def softmax(n):
                rows = p1[:, :, 0:S]
                ve.wait_ge(s1_sb, due(s1_sb, 4 * n + 4))
                ve.tensor_reduce(sm[:, 0, :], rows, AX.X, ALU.max).then_inc(soft, 1)
                ve.wait_ge(soft, due(soft, 2 * n + 1))
                ve.tensor_tensor(rows, rows, sm[:, 0, :].unsqueeze(2).to_broadcast([128, R * G, S]), ALU.subtract)\
                    .then_inc(soft, 1)

            def softmax_end(n):
                rows = p1[:, :, 0:S]
                ve.wait_ge(soft_e, due(soft_e, n + 1))
                ve.tensor_reduce(sm[:, 1, :], rows, AX.X, ALU.add).then_inc(soft_n, 1)
                ve.wait_ge(soft_n, due(soft_n, 3 * n + 1))
                ve.reciprocal(sm[:, 2, :], sm[:, 1, :]).then_inc(soft_n, 1)
                ve.wait_ge(soft_n, due(soft_n, 3 * n + 2))
                ve.tensor_tensor(rows, rows, sm[:, 2, :].unsqueeze(2).to_broadcast([128, R * G, S]), ALU.mult)\
                    .then_inc(soft_n, 1)

            def first_norm(n):
                ve.wait_ge(x_in[n % 2], due(x_in[n % 2], 32 * (n // 2 + 1)))
                layer_norm(0, n, x_sb[:, n % 2, :], xn[:, :])

            def reduce_piece(b, p):
                unit = b * PIECES + p
                ve.wait_ge(mx_done, due(mx_done, unit + 1))
                ve.tensor_reduce(mx_p[:, p:p + 1], mx_ps[unit % 2][:, 0:KP], AX.X, ALU.max).then_inc(red_done, 1)

            def negated_maxima(b):
                ve.wait_ge(red_done, due(red_done, (b + 1) * PIECES))
                ve.tensor_reduce(nm[:, :], mx_p[:, :].rearrange("p (j k) -> p j k", k=3), AX.X, ALU.max, negate=True)\
                    .then_inc(nm_step, 1)
                ve.wait_ge(nm_step, due(nm_step, 3 * b + 1))
                if b:
                    ve.wait_ge(ps["MT"], due(ps["MT"], b))
                ve.tensor_copy(nm_hl[:, 0, :], nm[:, :]).then_inc(nm_step, 1)
                ve.wait_ge(nm_step, due(nm_step, 3 * b + 2))
                ve.tensor_tensor(nm_hl[:, 1, :], nm[:, :], nm_hl[:, 0, :].bitcast(F32), ALU.subtract)\
                    .then_inc(nm_step, 1)

            ve.memset(x_sb[:, :, :], 0.0).then_inc(dve_c, 1)
            ve.memset(vhat[:, :, :, :], 0.0)
            ve.memset(eps_col[:, :], EPS)
            ve.memset(minus_half[:, :], -0.5).then_inc(dve_c, 1)
            first_norm(0)
            ve.wait_ge(pool_c, due(pool_c, IDENT_MADE))
            ve.tensor_reduce(gmask[:, :], ident[:, :].rearrange("p (g d) -> p g d", d=HD), AX.X, ALU.add)
            ve.tensor_reduce(e8[:, :], ident[:, :].rearrange("p (a e) -> p e a", e=8), AX.X, ALU.add)\
                .then_inc(dve_c, 1)
            ve.wait_ge(dve_c, due(dve_c, 3))
            step("KV", 0)
            step("A", 0)
            ve.wait_ge(pool_c, due(pool_c, MASKS_MADE))
            for name in ("S0", "S1", "S2", "S3"):
                step(name, 0)
            ve.wait_ge(raw_in, due(raw_in, 16 * 3))
            ve.tensor_tensor(gkron[:, :, :], g8[:, :].unsqueeze(2).to_broadcast([128, PAIRS, 8]),
                             e8[:, :].unsqueeze(1).to_broadcast([128, PAIRS, 8]), ALU.mult).then_inc(dve_c, 1)
            softmax_end(0)
            for name in ("W1", "H0", "H1", "H2", "H3"):
                step(name, 0)

            def body(i):
                for g in range(2 * GROUPS):
                    part, gg = g // GROUPS, g % GROUPS
                    bm = 2 * i + part
                    if bm < B:
                        for p in range(SEVENTH[gg], SEVENTH[gg + 1]):
                            reduce_piece(bm, p)
                        if SEVENTH[gg + 1] == PIECES and SEVENTH[gg] < PIECES:
                            negated_maxima(bm)
                    if g == 0 and i + 1 < PAIRS:
                        first_norm(i + 1)
                    if g == 4 and i + 1 < PAIRS:
                        softmax_end(i + 1)
                    for name, n in steps_of(i, g):
                        step(name, n)

            run_bodies(ve, at, body)

        @block.gpsimd
        def _(po):
            at = [None]
            due = counter(at)

            def add_up(b, half, after):
                if 0 <= b < B:
                    base = (b * 2 + half) * ADDS
                    dst = acc[:, b // 2 % 2, b % 2, half * HALF:(half + 1) * HALF]
                for k in range(1, ADDS + 1):
                    if 0 <= b < B:
                        unit = (b * 2 + half) * 12 + k
                        po.wait_ge(exp_done, due(exp_done, unit + 1))
                        if k == 1:
                            first = p_ring[:, (unit - 1) % PR, :]
                        else:
                            po.wait_ge(acc_done, due(acc_done, base + k - 1))
                            first = dst
                        po.tensor_tensor(dst, first, p_ring[:, unit % PR, :], ALU.add).then_inc(acc_done, 1)
                    if k in after:
                        after[k]()

            def power(which, n):
                if not 0 <= n < PAIRS:
                    return
                po.wait_ge(ln[which], due(ln[which], 3 * n + 2 if which == 0 else 4 * n + 3))
                po.tensor_tensor(rstd[:, which, 0:1], mv[:, which, 1:2], eps_col[:, :], ALU.add)\
                    .then_inc(ln_eps[which], 1)
                po.wait_ge(ln_eps[which], due(ln_eps[which], n + 1))
                po.tensor_tensor(rstd[:, which, 1:2], rstd[:, which, 0:1], minus_half[:, :], ALU.pow)\
                    .then_inc(ln_pow[which], 1)

            made = [0]

            def make(instruction):
                made[0] += 1
                instruction.then_inc(pool_c, 1)
                po.wait_ge(pool_c, due(pool_c, made[0]))

            make(po.memset(ident[:, :], 0.0))
            make(po.affine_select(out=ident[:, :], in_=ident[:, :], compare_op=ALU.not_equal, fill=1.0,
                                  base=0, pattern=[[-1, 128]], channel_multiplier=1))
            assert made[0] == IDENT_MADE
            po.wait_ge(dve_c, due(dve_c, 2))
            power(0, 0)
            make(po.memset(cmask[:, :], 0.0))
            for h in range(2):
                half_mask = cmask[h * SLOT:(h + 1) * SLOT, :]
                make(po.affine_select(out=half_mask, in_=half_mask, compare_op=ALU.is_ge, fill=NEG, base=0,
                                      pattern=[[-1, S]], channel_multiplier=1))
            make(po.memset(p1[:, :, S:SLOT], 0.0))
            assert made[0] == MASKS_MADE
            make(po.memset(ones[:, :], 1.0))
            make(po.memset(y_t[:, :, :], 0.0))
            make(po.memset(cqt[64:96, :], 0.0))
            make(po.memset(wqk_sb[64:96, :, :, :], 0.0))
            make(po.memset(ax_t[64:96, :], 1.0))
            make(po.memset(b_sb[64:96, :], 0.0))
            assert made[0] == PADS_MADE
            make(po.memset(c_st[96:98, :, :].bitcast(F32), 1.0))
            assert made[0] == ALL_MADE
            power(1, 0)

            def body(i):
                power(0, i + 1)
                for half in range(2):
                    add_up(2 * i - 1, half, {})
                add_up(2 * i, 0, {7: lambda: power(1, i + 1)})
                add_up(2 * i, 1, {4: lambda: power(2, i - 1)})

            run_bodies(po, at, body)


def kernel(**inputs):
    import numpy as np
    import concourse.bacc as bacc
    from concourse.bass_utils import run_bass_kernel_spmd

    a = {k: np.asarray(v) for k, v in inputs.items()}
    arrays = {
        "x": a["x"].reshape(PAIRS, 2, S, D),
        "ctx_t": a["ctx_4096"].transpose(0, 2, 1),
        "wq": a["L0_attn_wq"].reshape(D, G, R, HD).transpose(0, 2, 1, 3).reshape(D, D),
        "wk": a["L0_attn_wk"],
        "wv": a["L0_attn_wv"],
        "wo": a["L0_attn_wo"].reshape(G, R, HD, D).transpose(1, 0, 2, 3).reshape(D, D),
        "wq_d": a["L0_xattn_Wq_d"],
        "w_qk": a["L0_xattn_W_qk"],
        "wkv_d": a["L0_xattn_Wkv_d"],
        "wv_u": a["L0_xattn_Wv_u"],
        "gate_t": np.repeat(a["L0_ffn_gate"].transpose(1, 0), 8, axis=0),
        "kern": a["L0_ffn_kernel"],
        "bias": a["L0_ffn_bias"].reshape(1, D),
        "lora_a": a["L0_ffn_lora_A"].transpose(0, 2, 1),
        "lora_b": a["L0_ffn_lora_B"].transpose(0, 2, 1),
        "lora_as": a["L0_ffn_lora_A_shared"].transpose(1, 0),
        "lora_bs": a["L0_ffn_lora_B_shared"].transpose(1, 0),
    }
    nc = bacc.Bacc("TRN2", target_bir_lowering=False, num_devices=1, dynamic_dma_scratch_size=1024)
    ins, feed = {}, {}
    for name, value in arrays.items():
        value = np.ascontiguousarray(value)
        feed[f"in_{name}"] = value
        ins[name] = nc.dram_tensor(f"in_{name}", value.shape, mybir.dt.from_np(value.dtype), kind="ExternalInput").ap()
    out = nc.dram_tensor("out_y", (PAIRS, 2, S, D), F32, kind="ExternalOutput").ap()
    decoder_layer(nc, **ins, out=out)
    result = run_bass_kernel_spmd(nc, [feed], core_ids=[0])
    return result.results[0]["out_y"].reshape(B, S, D)
```

```python
from contextlib import ExitStack

import concourse.bass as bass
from concourse import mybir

F32 = mybir.dt.float32
F32R = mybir.dt.float32r
ALU = mybir.AluOpType
ACT = mybir.ActivationFunctionType
AX = mybir.AxisListType

B, S, D = 16, 56, 512
PAIRS = B // 2
SLOT = 64
CH = D // 128
G, R, HD = 8, 4, 16
H, L = 16, 32
LQ = D // 8
NK = 1500
KT = NK // 4
KC = 125
KG = KT // KC
HN = H * S
HALF = HN // 2
ROWT = HN // 128
KP = NK // 3
PIECES = ROWT * 3
RANK, NL = 32, 16
EPS = 1e-5
NEG = -1e30
PR = 8
STB = 3
GROUPS = 2 * KG
ADDS = 4 * KG - 1
LOOP_BODIES = 2
FIRST_LOOPED, LAST_LOOPED = 1, 6
IDENT_MADE, MASKS_MADE, PADS_MADE, ALL_MADE = 2, 6, 12, 14

PIECES_IN = [3, 3, 3, 3, 0, 0, 0, 3, 3, 3, 3, 0]
STEPS = [
    [("L0", "n"), ("A", "a"), ("N0", "n"), ("M", 2), ("T1", "n")],
    [("CT", "a"), ("M", 1), ("K", "n"), ("M", 2)],
    [("Q1", "n"), ("M", 3)],
    [("S0", "n"), ("M", 1), ("S1", "n"), ("S2", "n"), ("S3", "n")],
    [("MT", "m"), ("SE0", "n"), ("A", "b"), ("SE1", "n"), ("SN0", "n")],
    [("CT", "b"), ("SN1", "n")],
    [("V", "n"), ("P0", "n"), ("P1", "n"), ("P2", "n"), ("P3", "n"), ("XC", "f"), ("M", 2)],
    [("O1", "n"), ("Y", "f"), ("M", 2)],
    [("W1", "n"), ("M", 1), ("DN", "f"), ("N1", "n"), ("YT", "f"), ("M", 1), ("N2", "f")],
    [("T2", "n"), ("CQ", "n"), ("M", 2)],
    [("T3", "f"), ("H0", "n"), ("M", 1), ("H1", "n"), ("F1", "f")],
    [("MT", "o"), ("F2", "f"), ("H2", "n"), ("H3", "n")],
]
BANK = {"A": (0, 1), "T1": 0, "CT": (0, 1), "K": 0, "Q1": 1, "S0": 0, "S1": 1, "S2": 0, "S3": 1, "MT": 1,
        "V": 1, "P0": 0, "P1": 1, "P2": 0, "P3": 1, "O1": 0, "Y": 1, "W1": 0, "DN": 1, "YT": 0,
        "T2": 1, "CQ": 0, "T3": 1, "H0": 0, "H1": 1, "F1": 0, "F2": 0, "H2": 1, "H3": 0}


def steps_of(i, g):
    done = sum(PIECES_IN[g // GROUPS * GROUPS:g + 1])
    done += sum(w for h in range(g // GROUPS * GROUPS, g) for name, w in STEPS[h] if name == "M")
    for name, w in STEPS[g]:
        if name == "M":
            if 2 * i + g // GROUPS < B:
                yield name, range(done, done + w)
            done += w
            continue
        n = {"n": i + 1, "f": i - 1, "a": 2 * i + 1, "b": 2 * i + 2, "m": 2 * i, "o": 2 * i + 1}[w]
        if 0 <= n < (PAIRS if w in "nf" else B):
            yield name, n


def pieces_within(g):
    done = sum(PIECES_IN[g // GROUPS * GROUPS:g])
    done += sum(w for h in range(g // GROUPS * GROUPS, g) for name, w in STEPS[h] if name == "M")
    return range(done, done + PIECES_IN[g])


def decoder_layer(nc, x, ctx_t, wq, wk, wv, wo, wq_d, w_qk, wkv_d, wv_u, gate_t, kern, bias,
                  lora_a, lora_b, lora_as, lora_bs, out):
    with ExitStack() as stack:
        rates = {}

        def sb(name, shape, dt=F32):
            return stack.enter_context(nc.sbuf_tensor(name, shape, dt))

        def bank(name):
            return stack.enter_context(nc.psum_tensor(name, [128, 512], F32))

        def sem(name, per_pair):
            s = stack.enter_context(nc.semaphore(name))
            rates[s.name] = per_pair * LOOP_BODIES
            return s

        ctx_sb = sb("ctx_sb", [128, 2, CH, NK])
        wq_sb = sb("wq_sb", [128, CH, D])
        wk_sb = sb("wk_sb", [128, CH, 128])
        wv_sb = sb("wv_sb", [128, CH, 128])
        wo_sb = sb("wo_sb", [128, R, D])
        wqd_sb = sb("wqd_sb", [128, CH, LQ])
        wkv_sb = sb("wkv_sb", [128, CH, L])
        wqk_sb = sb("wqk_sb", [96, H, 3, L])
        wvu_sb = sb("wvu_sb", [128, D])
        kern_sb = sb("kern_sb", [128, CH, D])
        a_sb = sb("a_sb", [128, CH, 2 * RANK])
        b_sb = sb("b_sb", [96, D])
        c_st = sb("c_st", [98, 4, NK], F32R)
        c_nat = sb("c_nat", [KC, 4, KG, 128])
        q_st = sb("q_st", [98, 2, 2, HN], F32R)
        p_ring = sb("p_ring", [KC, PR, HALF])
        acc = sb("acc", [KC, 2, H, 128])
        ox = sb("ox", [128, H, 2, S])
        p1 = sb("p1", [128, R * G, SLOT])
        p1t = sb("p1t", [128, G // 2, R, 128])
        x_sb = sb("x_sb", [128, 2, D])
        x2_sb = sb("x2_sb", [128, 2, D])
        xn = sb("xn", [128, D])
        x3 = sb("x3", [128, D])
        x3n = sb("x3n", [128, D])
        xnt = sb("xnt", [128, CH, 128])
        qt = sb("qt", [128, R, 128])
        khat = sb("khat", [128, 2, G, S])
        vhat = sb("vhat", [128, 2, G // 2, 2 * HD])
        cqt = sb("cqt", [96, 128])
        ct_f = sb("ct_f", [128, KT])
        ct_hl = sb("ct_hl", [128, 2, KT], F32R)
        mx_p = sb("mx_p", [128, PIECES])
        nm = sb("nm", [128, ROWT])
        nm_hl = sb("nm_hl", [128, 2, ROWT], F32R)
        m_t = sb("m_t", [2 * ROWT, 128])
        r_den = sb("r_den", [128, H])
        y_t = sb("y_t", [128, H // 4, 128])
        ax_t = sb("ax_t", [96, 128])
        sm = sb("sm", [128, 3, R * G])
        stats = sb("stats", [128, 3, 7])
        mv = sb("mv", [128, 3, 2])
        rstd = sb("rstd", [128, 3, 2])
        ident = sb("ident", [128, 128])
        ones = sb("ones", [128, 1])
        gmask = sb("gmask", [128, G])
        e8 = sb("e8", [128, 8])
        cmask = sb("cmask", [128, S])
        minus_half = sb("minus_half", [128, 1])
        eps_col = sb("eps_col", [128, 1])
        g8 = sb("g8", [128, PAIRS])
        gkron = sb("gkron", [128, PAIRS, 8])
        spare = ctx_sb[:, 1, :, :].rearrange("p c k -> p (c k)")
        lora_raw = [spare[:, 0:2048], spare[:, 2048:4096]]
        lora_eff = [p_ring[0:64, :, :].rearrange("p a b -> p (a b)"),
                    acc[0:64, :, :, :].rearrange("p a h s -> p (a h s)")]

        st_ps = [bank(f"st_ps{n}") for n in range(STB)]
        mx_ps = [bank(f"mx_ps{n}") for n in range(2)]
        pv_ps = bank("pv_ps")
        mi_ps = [bank(f"mi_ps{n}") for n in range(2)]

        a_eff = nc.dram_tensor("a_eff", [PAIRS, D, RANK], F32).ap()
        b_eff = nc.dram_tensor("b_eff", [PAIRS, RANK, D], F32).ap()

        x_in = [sem(f"x_in{n}", 16) for n in range(2)]
        ctx_in = [sem(f"ctx_in{n}", 16) for n in range(2)]
        ab_in = sem("ab_in", 32)
        for s in x_in + ctx_in:
            rates[s.name] = 32
        w_attn = sem("w_attn", 0)
        w_cross = sem("w_cross", 0)
        w_ffn = sem("w_ffn", 0)
        raw_in = sem("raw_in", 0)
        eff_out = sem("eff_out", 0)
        cst_in = [sem(f"cst_in{n}", 0) for n in range(4)]
        for s in cst_in:
            rates[s.name] = 16 * 12
        m_in = [sem(f"m_in{n}", 32) for n in range(2)]
        y_out = sem("y_out", 32)
        pool_c = sem("pool_c", 0)
        dve_c = sem("dve_c", 0)
        lora_ps = sem("lora_ps", 0)
        lora_sb = sem("lora_sb", 0)
        ln = [sem("ln0", 3), sem("ln1", 4), sem("ln2", 5)]
        ln_eps = [sem(f"ln_eps{n}", 1) for n in range(3)]
        x3_base = sem("x3_base", 1)
        ln_pow = [sem(f"ln_pow{n}", 1) for n in range(3)]
        st_done = sem("st_done", 48)
        exp_done = sem("exp_done", 48)
        pv_done = sem("pv_done", 12)
        ox_sb = sem("ox_sb", 4)
        acc_done = sem("acc_done", 4 * ADDS)
        mx_done = sem("mx_done", 2 * PIECES)
        red_done = sem("red_done", 2 * PIECES)
        nm_step = sem("nm_step", 2 * 3)
        ps = {}
        for name in BANK:
            ps[name] = sem("ps_" + name, 2 if name in ("A", "CT", "MT") else 1)
        t1_sb = sem("t1_sb", 1)
        k_sb = sem("k_sb", 2)
        v_sb = sem("v_sb", 4)
        q1_sb = sem("q1_sb", 1)
        s1_sb = sem("s1_sb", 4)
        soft = sem("soft", 4)
        soft_e = sem("soft_e", 2)
        soft_n = sem("soft_n", 6)
        pt_sb = sem("pt_sb", 4)
        o1_sb = sem("o1_sb", 1)
        t2_sb = sem("t2_sb", 1)
        cq_sb = sem("cq_sb", 1)
        qh_hi = sem("qh_hi", 4)
        qh_lo = sem("qh_lo", 4)
        a_f = sem("a_f", 2)
        a_hi = sem("a_hi", 2)
        a_lo = sem("a_lo", 2)
        ct_sb = sem("ct_sb", 2)
        mt_sb = sem("mt_sb", 2)
        yu_sb = sem("yu_sb", 1)
        r_sb = sem("r_sb", 1)
        t3_sb = sem("t3_sb", 1)
        f1_sb = sem("f1_sb", 1)
        f2_sb = sem("f2_sb", 1)

        def step_bank(name, n):
            b = BANK[name]
            return mi_ps[b[n % 2] if isinstance(b, tuple) else b]

        def lora_bank(q):
            return [*st_ps, *mx_ps, pv_ps][q % 6]

        block = stack.enter_context(nc.Block())

        def counter(at):
            def due(s, count):
                assert count > 0
                return count if at[0] is None else at[0] * rates[s.name] + count
            return due

        def run_bodies(eng, at, body):
            body(0)
            with eng.Fori(0, (LAST_LOOPED - FIRST_LOOPED + 1) // LOOP_BODIES) as rnd:
                at[0] = rnd
                for i in range(FIRST_LOOPED, FIRST_LOOPED + LOOP_BODIES):
                    body(i)
                at[0] = None
            for i in range(LAST_LOOPED + 1, PAIRS + 1):
                body(i)

        @block.sync
        def _(sp):
            at = [None]
            due = counter(at)
            dma = sp.dma_start

            def pair_index(n):
                return n if at[0] is None else at[0] * LOOP_BODIES + n

            def batch_index(b):
                return b if at[0] is None else at[0] * (2 * LOOP_BODIES) + b

            def load_x(n):
                if n >= 2:
                    sp.wait_ge(ln[1], due(ln[1], 4 * (n - 2) + 1))
                for h in range(2):
                    dma(x_sb[h * SLOT:h * SLOT + S, n % 2, :], x[pair_index(n), h]).then_inc(x_in[n % 2], 16)

            def load_ctx(b):
                if b >= 2:
                    sp.wait_ge(ps["A"], due(ps["A"], b - 1))
                dma(ctx_sb[:, b % 2, :, :],
                    ctx_t[batch_index(b)].rearrange("(p c) k -> p c k", c=CH)).then_inc(ctx_in[b % 2], 16)

            def load_ab(n):
                dma(a_sb[:, :, 0:RANK],
                    a_eff[pair_index(n)].rearrange("(c p) r -> p c r", p=128)).then_inc(ab_in, 16)
                dma(b_sb[0:RANK, :], b_eff[pair_index(n)]).then_inc(ab_in, 16)

            def spread_ct(b):
                for part, dst in ((0, 0), (1, L), (0, 2 * L)):
                    if dst == 0:
                        sp.wait_ge(a_hi, due(a_hi, b + 1))
                    if dst == L:
                        sp.wait_ge(a_lo, due(a_lo, b + 1))
                    for t in range(4):
                        dma(c_st[dst:dst + L, b % 4, t * KT:(t + 1) * KT].bitcast(F32),
                            ct_hl[t * L:(t + 1) * L, part, :].bitcast(F32)).then_inc(cst_in[b % 4], 16)

            def spread_m(b):
                sp.wait_ge(mt_sb, due(mt_sb, b + 1))
                for part in range(2):
                    dma(q_st[96 + part:97 + part, b // 2 % 2, b % 2, :].bitcast(F32)
                        .rearrange("a (j p) -> a j p", p=128),
                        m_t[part * ROWT:(part + 1) * ROWT, :]).then_inc(m_in[b % 2], 16)

            def store_y(n):
                sp.wait_ge(f2_sb, due(f2_sb, n + 1))
                for h in range(2):
                    dma(out[pair_index(n), h], x3n[h * SLOT:h * SLOT + S, :]).then_inc(y_out, 16)

            sp.wait_ge(dve_c, due(dve_c, 1))
            load_x(0)
            for c in range(2):
                dma(wq_sb[:, 2 * c:2 * c + 2, :], wq[c * 256:(c + 1) * 256, :].rearrange("(c p) n -> p c n", p=128))\
                    .then_inc(w_attn, 16)
            dma(wk_sb[:, :, :], wk.rearrange("(c p) n -> p c n", p=128)).then_inc(w_attn, 16)
            dma(wv_sb[:, :, :], wv.rearrange("(c p) n -> p c n", p=128)).then_inc(w_attn, 16)
            dma(wkv_sb[:, :, :], wkv_d.rearrange("(p c) n -> p c n", c=CH)).then_inc(w_cross, 16)
            load_ctx(0)
            dma(wo_sb[:, :, :], wo.rearrange("(r p) n -> p r n", p=128)).then_inc(w_attn, 16)
            dma(wqd_sb[:, :, :], wq_d.rearrange("(c p) n -> p c n", p=128)).then_inc(w_cross, 16)
            for k in range(3):
                dma(wqk_sb[0:LQ, :, k, :], w_qk.rearrange("p (h l) -> p h l", l=L)).then_inc(w_cross, 16)
            for t in range(4):
                dma(wvu_sb[t * L:(t + 1) * L, :], wv_u).then_inc(w_cross, 16)
            for k in range(2):
                dma(lora_raw[k], (lora_a, lora_b)[k].rearrange("n (e f) r -> (n e) (f r)", e=8)).then_inc(raw_in, 16)
            dma(g8[:, :], gate_t).then_inc(raw_in, 16)
            spread_ct(0)
            sp.wait_ge(lora_ps, due(lora_ps, 8))
            load_ctx(1)
            dma(kern_sb[:, :, :], kern.rearrange("(c p) n -> p c n", p=128)).then_inc(w_ffn, 16)
            sp.wait_ge(pool_c, due(pool_c, PADS_MADE))
            dma(a_sb[:, :, RANK:2 * RANK], lora_as.rearrange("(c p) r -> p c r", p=128)).then_inc(w_ffn, 16)
            dma(b_sb[RANK:2 * RANK, :], lora_bs).then_inc(w_ffn, 16)
            dma(b_sb[2 * RANK:2 * RANK + 1, :], bias).then_inc(y_out, 16)
            sp.wait_ge(eff_out, due(eff_out, 32))

            def body(i):
                if 2 * i + 2 < B:
                    load_x(i + 1)
                    load_ctx(2 * i + 2)
                for g in range(2 * GROUPS):
                    for name, n in steps_of(i, g):
                        if name == "A":
                            spread_ct(n)
                            if n % 2 and n + 2 < B:
                                load_ctx(n + 2)
                        elif name == "MT":
                            spread_m(n)
                        elif name == "Y":
                            load_ab(n)
                        elif name == "F2":
                            store_y(n)

            run_bodies(sp, at, body)
            sp.wait_ge(y_out, due(y_out, 32 * PAIRS + 16))

        @block.tensor
        def _(pe):
            at = [None]
            due = counter(at)
            mm = pe.matmul

            def four_transposes(bank_, src):
                for c in range(4):
                    last = pe.transpose(bank_[:, c * 128:(c + 1) * 128], src[:, c * 128:(c + 1) * 128], ident[:, :])
                return last

            def step(name, n, i=0, g=0):
                if name == "M":
                    for p in n:
                        maxima(2 * i + g // GROUPS, p)
                if name not in BANK:
                    return
                o = step_bank(name, n)
                slot = n % 2
                if name == "T1":
                    if n:
                        pe.wait_ge(qh_lo, due(qh_lo, 4 * n))
                    pe.wait_ge(ln[0], due(ln[0], 3 * n + 3))
                    last = four_transposes(o, xn)
                elif name == "K":
                    pe.wait_ge(t1_sb, due(t1_sb, n + 1))
                    for c in range(CH):
                        last = mm(o[:, 0:128], wk_sb[:, c, :], xnt[:, c, :], start=(c == 0), stop=(c == CH - 1))
                elif name == "V":
                    if n:
                        pe.wait_ge(mt_sb, due(mt_sb, 2 * n - 1))
                    for c in range(CH):
                        last = mm(o[:, 0:128], xnt[:, c, :], wv_sb[:, c, :], start=(c == 0), stop=(c == CH - 1))
                elif name == "Q1":
                    if n:
                        pe.wait_ge(ct_sb, due(ct_sb, 2 * n))
                    for r in range(R):
                        for c in range(CH):
                            last = mm(o[:, r * 128:(r + 1) * 128], wq_sb[:, c, r * 128:(r + 1) * 128],
                                      xnt[:, c, :], start=(c == 0), stop=(c == CH - 1))
                elif name in ("S0", "S1", "S2", "S3"):
                    r = int(name[1])
                    if r == 0:
                        pe.wait_ge(q1_sb, due(q1_sb, n + 1))
                        pe.wait_ge(k_sb, due(k_sb, 2 * n + 2))
                    if r >= 2:
                        pe.wait_ge(s1_sb, due(s1_sb, 4 * n + r - 1))
                    for b in range(2):
                        last = mm(o[b * SLOT:(b + 1) * SLOT, 0:G * S], qt[:, r, b * SLOT:(b + 1) * SLOT],
                                  khat[:, b, :, :].rearrange("p g k -> p (g k)"), start=True, stop=True)
                elif name in ("P0", "P1", "P2", "P3"):
                    r = int(name[1])
                    if r == 0:
                        pe.wait_ge(ct_sb, due(ct_sb, 2 * n + 1))
                    if r % 2 == 0:
                        pe.wait_ge(soft_n, due(soft_n, 6 * n + 3 * (r // 2) + 3))
                    if r == 1:
                        pe.wait_ge(v_sb, due(v_sb, 4 * n + 4))
                    if r >= 2:
                        pe.wait_ge(pt_sb, due(pt_sb, 4 * n + r - 1))
                    last = four_transposes(o, p1[:, r * G:(r + 1) * G, :].rearrange("p g k -> p (g k)"))
                elif name == "O1":
                    pe.wait_ge(pt_sb, due(pt_sb, 4 * n + 4))
                    for b in range(2):
                        for g in range(G // 2):
                            last = mm(o[g * 32:(g + 1) * 32, b * 256:(b + 1) * 256], vhat[:, b, g, :],
                                      p1t[:, g, :, b * SLOT:(b + 1) * SLOT], start=True, stop=True)
                elif name == "W1":
                    pe.wait_ge(o1_sb, due(o1_sb, n + 1))
                    for r in range(R):
                        last = mm(o[:, :], qt[:, r, :], wo_sb[:, r, :], start=(r == 0), stop=(r == R - 1))
                elif name == "T2":
                    if n >= 2:
                        pe.wait_ge(r_sb, due(r_sb, n - 1))
                    pe.wait_ge(ln[1], due(ln[1], 4 * n + 4))
                    last = four_transposes(o, xn)
                elif name == "CQ":
                    if n >= 2:
                        pe.wait_ge(ln[2], due(ln[2], 5 * n - 9))
                    pe.wait_ge(t2_sb, due(t2_sb, n + 1))
                    for c in range(CH):
                        last = mm(o[0:LQ, 0:128], wqd_sb[:, c, :], xnt[:, c, :], start=(c == 0), stop=(c == CH - 1))
                elif name in ("H0", "H1", "H2", "H3"):
                    k = int(name[1])
                    if k == 0:
                        pe.wait_ge(cq_sb, due(cq_sb, n + 1))
                    if k == 1 and n >= 2:
                        pe.wait_ge(t3_sb, due(t3_sb, n - 1))
                    if k == 2 and n:
                        pe.wait_ge(mt_sb, due(mt_sb, 2 * n))
                    if k == 2 and n == 0:
                        pe.wait_ge(qh_lo, due(qh_lo, 2))
                    if k == 3 and n < 2:
                        pe.wait_ge(qh_lo, due(qh_lo, 4 * n + 1))
                    if k == 3 and n >= 2:
                        pe.wait_ge(f2_sb, due(f2_sb, n - 1))
                    for h in range(4):
                        head = 4 * k + h
                        last = mm(o[0:96, h * 2 * S:(h + 1) * 2 * S], wqk_sb[:, head, :, :].rearrange("p k l -> p (k l)"),
                                  cqt[:, :].rearrange("p (b s) -> p b s", b=2)[:, :, 0:S], start=True, stop=True)
                elif name == "A":
                    if n % 2:
                        pe.wait_ge(qh_lo, due(qh_lo, 2 * n + 1))
                    elif n:
                        pe.wait_ge(s1_sb, due(s1_sb, 2 * n + 3))
                    pe.wait_ge(ctx_in[slot], due(ctx_in[slot], 16 * (n // 2 + 1)))
                    for c in range(CH):
                        for t in range(4):
                            last = mm(o[t * L:(t + 1) * L, 0:KT], wkv_sb[:, c, :],
                                      ctx_sb[:, slot, c, t * KT:(t + 1) * KT], start=(c == 0), stop=(c == CH - 1))
                elif name == "CT":
                    pe.wait_ge(a_f, due(a_f, n + 1))
                    for k in range(KG):
                        last = pe.transpose(o[0:KC, k * 128:(k + 1) * 128], ct_f[:, k * KC:(k + 1) * KC], ident[:, :])
                elif name == "MT":
                    if n % 2 == 0 and n + 2 < B:
                        pe.wait_ge(s1_sb, due(s1_sb, 2 * n + 8))
                    if n == B - 2:
                        pe.wait_ge(ct_sb, due(ct_sb, B))
                    if n % 2 and n + 1 < B:
                        pe.wait_ge(qh_lo, due(qh_lo, 2 * n + 4))
                    pe.wait_ge(nm_step, due(nm_step, 3 * n + 3))
                    last = pe.transpose(o[0:2 * ROWT, 0:128],
                                        nm_hl[:, :, :].rearrange("p a j -> p (a j)").bitcast(F32), ident[:, :])
                elif name == "Y":
                    if n >= PAIRS - 2:
                        pe.wait_ge(mt_sb, due(mt_sb, B - PAIRS + 1 + n))
                    pe.wait_ge(ox_sb, due(ox_sb, 4 * n + 4))
                    for h in range(H):
                        t, q = h % 4, h // 4
                        last = mm(o[t * 32:(t + 1) * 32, q * 2 * S:(q + 1) * 2 * S], wvu_sb[:, h * L:(h + 1) * L],
                                  ox[:, h, :, :].rearrange("p b s -> p (b s)"), start=True, stop=True)
                elif name == "DN":
                    pe.wait_ge(yu_sb, due(yu_sb, n + 1))
                    pe.wait_ge(acc_done, due(acc_done, 4 * ADDS * (n + 1)))
                    for h in range(H):
                        last = mm(o[:, h:h + 1], acc[:, slot, h, :], ones[0:KC, :], start=True, stop=True)
                elif name == "YT":
                    if n + 2 < PAIRS:
                        pe.wait_ge(ln[1], due(ln[1], 4 * n + 9))
                    elif n + 2 == PAIRS:
                        pe.wait_ge(qh_lo, due(qh_lo, 4 * PAIRS))
                    else:
                        pe.wait_ge(f2_sb, due(f2_sb, n))
                    pe.wait_ge(yu_sb, due(yu_sb, n + 1))
                    last = four_transposes(o, y_t[:, :, :].rearrange("p q s -> p (q s)"))
                elif name == "T3":
                    pe.wait_ge(ln[2], due(ln[2], 5 * n + 5))
                    last = four_transposes(o, x3n)
                elif name == "F1":
                    if n + 2 < PAIRS:
                        pe.wait_ge(qh_lo, due(qh_lo, 4 * n + 9))
                    pe.wait_ge(t3_sb, due(t3_sb, n + 1))
                    pe.wait_ge(ab_in, due(ab_in, 32 * (n + 1)))
                    for c in range(CH):
                        last = mm(o[0:2 * RANK, 0:128], a_sb[:, c, :], xnt[:, c, :],
                                  start=(c == 0), stop=(c == CH - 1))
                elif name == "F2":
                    pe.wait_ge(f1_sb, due(f1_sb, n + 1))
                    for c in range(CH):
                        mm(o[:, :], xnt[:, c, :], kern_sb[:, c, :], start=(c == 0), stop=False)
                    last = mm(o[:, :], ax_t[:, :], b_sb[:, :], start=False, stop=True)
                last.then_inc(ps[name], 1)

            def scores(b, g, t):
                unit = b * 24 + g * 4 + t
                half, k = g // KG, g % KG
                if g == 0 and t == 0:
                    pe.wait_ge(m_in[b % 2], due(m_in[b % 2], 32 * (b // 2 + 1)))
                if unit >= STB:
                    pe.wait_ge(exp_done, due(exp_done, unit - STB + 1))
                mm(st_ps[unit % STB][0:KC, 0:HALF], c_st[:, b % 4, t * KT + k * KC:t * KT + (k + 1) * KC],
                   q_st[:, b // 2 % 2, b % 2, half * HALF:(half + 1) * HALF],
                   start=True, stop=True).then_inc(st_done, 1)

            def sums(b, g):
                half, k = g // KG, g % KG
                pe.wait_ge(exp_done, due(exp_done, b * 24 + g * 4 + 4))
                if g == 0:
                    pe.wait_ge(ct_sb, due(ct_sb, b + 1))
                if k == 0 and b * 2 + half:
                    pe.wait_ge(ox_sb, due(ox_sb, b * 2 + half))
                for t in range(4):
                    unit = b * 24 + g * 4 + t
                    last = mm(pv_ps[t * L:(t + 1) * L, 0:HALF], c_nat[:, b % 4, k, t * L:(t + 1) * L],
                              p_ring[:, unit % PR, :], start=(k == 0), stop=(k == KG - 1))
                last.then_inc(pv_done, 1)

            def maxima(b, p):
                j, k = p // 3, p % 3
                if p == 0:
                    pe.wait_ge(cst_in[b % 4], due(cst_in[b % 4], 16 * 12 * (b // 4 + 1)))
                if k == 0:
                    pe.wait_ge(qh_lo, due(qh_lo, 4 * (b // 2) + ((j + 1) * 128 - 1) // (4 * S) + 1))
                if b * PIECES + p >= 2:
                    pe.wait_ge(red_done, due(red_done, b * PIECES + p - 1))
                mm(mx_ps[(b * PIECES + p) % 2][:, 0:KP], q_st[0:96, b // 2 % 2, b % 2, j * 128:(j + 1) * 128],
                   c_st[0:96, b % 4, k * KP:(k + 1) * KP], start=True, stop=True).then_inc(mx_done, 1)

            def lora_factors():
                pe.wait_ge(raw_in, due(raw_in, 16 * 3))
                pe.wait_ge(dve_c, due(dve_c, 4))
                for q in range(8):
                    if q >= 6:
                        pe.wait_ge(lora_sb, due(lora_sb, q - 5))
                    mm(lora_bank(q)[0:64, :], gkron[:, :, :].rearrange("p i e -> p (i e)"),
                       lora_raw[q // 4][:, q % 4 * 512:(q % 4 + 1) * 512], start=True, stop=True)\
                        .then_inc(lora_ps, 1)

            pe.wait_ge(pool_c, due(pool_c, IDENT_MADE))
            step("T1", 0)
            pe.wait_ge(w_attn, due(w_attn, 16 * 5))
            step("K", 0)
            step("Q1", 0)
            pe.wait_ge(w_cross, due(w_cross, 16 * 9))
            pe.wait_ge(dve_c, due(dve_c, 3))
            pe.wait_ge(pool_c, due(pool_c, PADS_MADE))
            pe.wait_ge(k_sb, due(k_sb, 2))
            step("A", 0)
            pe.wait_ge(a_f, due(a_f, 1))
            for name in ("S0", "S1", "S2", "S3"):
                step(name, 0)
            pe.wait_ge(s1_sb, due(s1_sb, 4))
            step("V", 0)
            step("CT", 0)
            lora_factors()
            for name in ("P0", "P1", "P2", "P3", "O1", "W1", "T2", "CQ", "H0", "H1", "H2", "H3"):
                step(name, 0)
            pe.wait_ge(w_ffn, due(w_ffn, 16 * 3))
            pe.wait_ge(y_out, due(y_out, 16))
            pe.wait_ge(lora_sb, due(lora_sb, 8))
            pe.wait_ge(pool_c, due(pool_c, ALL_MADE))

            def body(i):
                for g in range(2 * GROUPS):
                    part, gg = g // GROUPS, g % GROUPS
                    bs, bm = 2 * i - 1 + part, 2 * i + part
                    todo = pieces_within(g) if bm < B else []
                    for t in range(4):
                        if 0 <= bs < B:
                            scores(bs, gg, t)
                        for p in todo[t:t + 1]:
                            maxima(bm, p)
                    bl, gl = (bs, gg - 1) if gg else (bs - 1, GROUPS - 1)
                    if 0 <= bl < B:
                        sums(bl, gl)
                    for name, n in steps_of(i, g):
                        step(name, n, i, g)

            run_bodies(pe, at, body)

        @block.scalar
        def _(act):
            at = [None]
            due = counter(at)

            def copy(dst, src, scale=1.0):
                return act.activation(dst, src, ACT.Copy, scale=scale)

            def step(name, n, i=0, g=0):
                if name == "XC":
                    act.wait_ge(ln[1], due(ln[1], 4 * n + 4))
                    if n + 2 >= PAIRS:
                        act.wait_ge(f2_sb, due(f2_sb, n))
                    copy(x3[:, :], x2_sb[:, n % 2, :]).then_inc(x3_base, 1)
                    return
                if name not in ("T1", "V", "Q1", "P0", "P1", "P2", "P3", "SE0", "SE1", "O1", "T2", "CQ", "H0", "H1", "H2",
                                "H3", "A", "CT", "MT", "Y", "T3", "F1"):
                    return
                if name in ("SE0", "SE1"):
                    k = int(name[2])
                    rows = p1[:, k * 2 * G:(k + 1) * 2 * G, 0:S]
                    act.wait_ge(soft, due(soft, 4 * n + 2 * k + 2))
                    act.activation(rows, rows, ACT.Exp).then_inc(soft_e, 1)
                    return
                o = step_bank(name, n)
                act.wait_ge(ps[name], due(ps[name], n + 1))
                if name == "T1":
                    copy(xnt[:, :, :].rearrange("p c s -> p (c s)"), o[:, :]).then_inc(t1_sb, 1)
                elif name == "V":
                    for b in range(2):
                        for h in range(2):
                            src = o[b * SLOT:(b + 1) * SLOT, 0:128].rearrange("p (g e d) -> p g e d", g=4, e=2)
                            copy(vhat[h * 64:(h + 1) * 64, b, :, h * HD:(h + 1) * HD], src[:, :, h, :])\
                                .then_inc(v_sb, 1)
                elif name == "Q1":
                    copy(qt[:, :, :].rearrange("p r s -> p (r s)"), o[:, :], scale=float(HD) ** -0.5)\
                        .then_inc(q1_sb, 1)
                elif name[0] == "P":
                    copy(p1t[:, :, int(name[1]), :], o[:, :].rearrange("p (g s) -> p g s", g=4)).then_inc(pt_sb, 1)
                elif name == "O1":
                    copy(qt[:, :, :].rearrange("p r (b s) -> p b r s", b=2),
                         o[:, :].rearrange("p (b r s) -> p b r s", b=2, r=R)).then_inc(o1_sb, 1)
                elif name == "T2":
                    copy(xnt[:, :, :].rearrange("p c s -> p (c s)"), o[:, :]).then_inc(t2_sb, 1)
                elif name == "CQ":
                    copy(cqt[0:LQ, :], o[0:LQ, 0:128]).then_inc(cq_sb, 1)
                elif name[0] == "H":
                    k = int(name[1])
                    if n >= 2:
                        act.wait_ge(st_done, due(st_done, 24 * (2 * n - 2)))
                    for b in range(2):
                        last = copy(q_st[0:96, n % 2, b, k * 4 * S:(k + 1) * 4 * S].rearrange("p (h s) -> p h s", h=4),
                                    o[0:96, 0:448].rearrange("p (h b s) -> p b h s", b=2, s=S)[:, b])
                    last.then_inc(qh_hi, 1)
                elif name == "A":
                    if n:
                        act.wait_ge(a_lo, due(a_lo, n))
                    copy(ct_f[:, :], o[:, 0:KT]).then_inc(a_f, 1)
                elif name == "CT":
                    copy(c_nat[:, n % 4, :, :].rearrange("p k l -> p (k l)"), o[0:KC, 0:KG * 128])\
                        .then_inc(ct_sb, 1)
                elif name == "MT":
                    if n:
                        act.wait_ge(m_in[(n - 1) % 2], due(m_in[(n - 1) % 2], 32 * ((n - 1) // 2 + 1)))
                    copy(m_t[:, :], o[0:2 * ROWT, 0:128]).then_inc(mt_sb, 1)
                elif name == "Y":
                    copy(y_t[:, :, :].rearrange("p q (b s) -> p q b s", b=2)[:, :, :, 0:S],
                         o[:, 0:448].rearrange("p (q b s) -> p q b s", q=4, b=2)).then_inc(yu_sb, 1)
                elif name == "T3":
                    copy(xnt[:, :, :].rearrange("p c s -> p (c s)"), o[:, :]).then_inc(t3_sb, 1)
                elif name == "F1":
                    copy(ax_t[0:2 * RANK, :], o[0:2 * RANK, 0:128]).then_inc(f1_sb, 1)

            def exponentials(b, g):
                half = g // KG
                for t in range(4):
                    unit = b * 24 + g * 4 + t
                    act.wait_ge(st_done, due(st_done, unit + 1))
                    old = unit - PR
                    if old >= 0:
                        act.wait_ge(pv_done, due(pv_done, old // 4 + 1))
                        act.wait_ge(acc_done, due(acc_done, old // 12 * ADDS + max(old % 12, 1)))
                    act.activation(p_ring[:, unit % PR, :], st_ps[unit % STB][0:KC, 0:HALF], ACT.Exp,
                                   scale=float(L) ** -0.5).then_inc(exp_done, 1)

            def out_of_sums(b, half):
                act.wait_ge(pv_done, due(pv_done, b * 6 + half * KG + KG))
                if b % 2 == 0 and half == 0 and b:
                    act.wait_ge(ps["Y"], due(ps["Y"], b // 2))
                copy(ox[:, half * 8:half * 8 + 8, b % 2, :],
                     pv_ps[:, 0:HALF].rearrange("p (h s) -> p h s", h=8)).then_inc(ox_sb, 1)

            act.wait_ge(dve_c, due(dve_c, 2))
            for name in ("T1", "Q1", "A", "V", "CT", "SE0", "SE1"):
                step(name, 0)
            for q in range(8):
                act.wait_ge(lora_ps, due(lora_ps, q + 1))
                copy(lora_eff[q // 4][:, q % 4 * 512:(q % 4 + 1) * 512], lora_bank(q)[0:64, :]).then_inc(lora_sb, 1)
            act.wait_ge(lora_sb, due(lora_sb, 8))
            for k, dst in enumerate((a_eff, b_eff)):
                act.dma_start(dst.rearrange("i (e f) r -> (i e) (f r)", e=8), lora_eff[k][:, 0:2048])\
                    .then_inc(eff_out, 16)
            for name in ("P0", "P1", "P2", "P3", "O1", "T2", "CQ", "H0", "H1", "H2", "H3"):
                step(name, 0)
            act.wait_ge(eff_out, due(eff_out, 32))

            def body(i):
                for g in range(2 * GROUPS):
                    part, gg = g // GROUPS, g % GROUPS
                    bs = 2 * i - 1 + part
                    if 0 <= bs < B:
                        exponentials(bs, gg)
                    bl, gl = (bs, gg - 1) if gg else (bs - 1, GROUPS - 1)
                    if 0 <= bl < B and gl % KG == KG - 1:
                        out_of_sums(bl, gl // KG)
                    for name, n in steps_of(i, g):
                        step(name, n, i, g)

            run_bodies(act, at, body)

        @block.vector
        def _(ve):
            at = [None]
            due = counter(at)

            def statistics(which, n, src):
                s = ln[which]
                k = (3 * n, 4 * n + 1, 5 * n + 2)[which]
                ve.bn_stats(stats[:, which, 0:6], src).then_inc(s, 1)
                ve.wait_ge(s, due(s, k + 1))
                ve.tensor_copy(stats[:, which, 6:7], eps_col[:, :])
                ve.bn_aggr(mv[:, which, :], stats[:, which, 0:6]).then_inc(s, 1)

            def normalise(which, n, src, dst):
                ve.wait_ge(ln_pow[which], due(ln_pow[which], n + 1))
                ve.tensor_scalar(dst, src, mv[:, which, 0:1], rstd[:, which, 1:2], ALU.subtract, ALU.mult)\
                    .then_inc(ln[which], 1)

            def step(name, n, i=0, g=0):
                if name == "M":
                    for p in n:
                        reduce_piece(2 * i + g // GROUPS, p)
                    return
                slot = n % 2
                if name == "L0":
                    ve.wait_ge(x_in[slot], due(x_in[slot], 32 * (n // 2 + 1)))
                    statistics(0, n, x_sb[:, slot, :])
                elif name == "N0":
                    normalise(0, n, x_sb[:, slot, :], xn[:, :])
                elif name == "N1":
                    normalise(1, n, x2_sb[:, slot, :], xn[:, :])
                elif name == "N2":
                    normalise(2, n, x3[:, :], x3n[:, :])
                elif name in ("SN0", "SN1"):
                    softmax_end(n, int(name[2]))
                if name not in BANK:
                    return
                o = step_bank(name, n)
                if name in ("K", "S0", "S1", "S2", "S3", "W1", "H0", "H1", "H2", "H3", "DN", "YT", "F2"):
                    ve.wait_ge(ps[name], due(ps[name], n + 1))
                if name == "K":
                    for b in range(2):
                        k = o[:, b * SLOT:b * SLOT + S].unsqueeze(1).to_broadcast([128, G, S])
                        ve.tensor_tensor(khat[:, b, :, :], k, gmask[:, :].unsqueeze(2).to_broadcast([128, G, S]),
                                         ALU.mult).then_inc(k_sb, 1)
                elif name in ("S0", "S1", "S2", "S3"):
                    r = int(name[1])
                    ve.tensor_tensor(p1[:, r * G:(r + 1) * G, 0:S], o[:, 0:G * S].rearrange("p (g k) -> p g k", g=G),
                                     cmask[:, :].unsqueeze(1).to_broadcast([128, G, S]), ALU.add)\
                        .then_inc(s1_sb, 1)
                    if r % 2:
                        softmax(n, r // 2)
                elif name == "W1":
                    if n >= 2:
                        ve.wait_ge(x3_base, due(x3_base, n - 1))
                    ve.tensor_tensor(x2_sb[:, slot, :], o[:, :], x_sb[:, slot, :], ALU.add).then_inc(ln[1], 1)
                    ve.wait_ge(ln[1], due(ln[1], 4 * n + 1))
                    statistics(1, n, x2_sb[:, slot, :])
                elif name[0] == "H":
                    k = int(name[1])
                    ve.wait_ge(qh_hi, due(qh_hi, 4 * n + k + 1))
                    for b in range(2):
                        q = q_st[64:96, slot, b, k * 4 * S:(k + 1) * 4 * S].rearrange("p (h s) -> p h s", h=4)
                        last = ve.tensor_tensor(q, o[64:96, 0:448].rearrange("p (h b s) -> p b h s", b=2, s=S)[:, b],
                                                q.bitcast(F32), ALU.subtract)
                    last.then_inc(qh_lo, 1)
                elif name == "A":
                    if n:
                        ve.wait_ge(cst_in[(n - 1) % 4], due(cst_in[(n - 1) % 4], 16 * 12 * ((n - 1) // 4 + 1)))
                    ve.wait_ge(a_f, due(a_f, n + 1))
                    ve.tensor_copy(ct_hl[:, 0, :], ct_f[:, :]).then_inc(a_hi, 1)
                    ve.wait_ge(a_hi, due(a_hi, n + 1))
                    ve.tensor_tensor(ct_hl[:, 1, :], ct_f[:, :], ct_hl[:, 0, :].bitcast(F32), ALU.subtract)\
                        .then_inc(a_lo, 1)
                elif name == "DN":
                    ve.reciprocal(r_den[:, :], o[:, 0:H]).then_inc(r_sb, 1)
                elif name == "YT":
                    ve.wait_ge(y_out, due(y_out, 32 * n + 16))
                    ve.wait_ge(r_sb, due(r_sb, n + 1))
                    ve.tensor_tensor(x3n[:, :].rearrange("p (h d) -> p h d", d=L), o[:, :].rearrange("p (h d) -> p h d", d=L),
                                     r_den[:, :].unsqueeze(2).to_broadcast([128, H, L]), ALU.mult).then_inc(ln[2], 1)
                    ve.wait_ge(ln[2], due(ln[2], 5 * n + 1))
                    ve.wait_ge(x3_base, due(x3_base, n + 1))
                    ve.tensor_tensor(x3[:, :], x3n[:, :], x3[:, :], ALU.add).then_inc(ln[2], 1)
                    ve.wait_ge(ln[2], due(ln[2], 5 * n + 2))
                    statistics(2, n, x3[:, :])
                elif name == "F2":
                    ve.tensor_tensor(x3n[:, :], o[:, :], x3[:, :], ALU.add).then_inc(f2_sb, 1)

            def softmax(n, k):
                rows = p1[:, k * 2 * G:(k + 1) * 2 * G, 0:S]
                most = sm[:, 0, k * 2 * G:(k + 1) * 2 * G]
                ve.wait_ge(s1_sb, due(s1_sb, 4 * n + 2 * k + 2))
                ve.tensor_reduce(most, rows, AX.X, ALU.max).then_inc(soft, 1)
                ve.wait_ge(soft, due(soft, 4 * n + 2 * k + 1))
                ve.tensor_tensor(rows, rows, most.unsqueeze(2).to_broadcast([128, 2 * G, S]), ALU.subtract)\
                    .then_inc(soft, 1)

            def softmax_end(n, k):
                rows = p1[:, k * 2 * G:(k + 1) * 2 * G, 0:S]
                total, inverse = (sm[:, j, k * 2 * G:(k + 1) * 2 * G] for j in (1, 2))
                ve.wait_ge(soft_e, due(soft_e, 2 * n + k + 1))
                ve.tensor_reduce(total, rows, AX.X, ALU.add).then_inc(soft_n, 1)
                ve.wait_ge(soft_n, due(soft_n, 6 * n + 3 * k + 1))
                ve.reciprocal(inverse, total).then_inc(soft_n, 1)
                ve.wait_ge(soft_n, due(soft_n, 6 * n + 3 * k + 2))
                ve.tensor_tensor(rows, rows, inverse.unsqueeze(2).to_broadcast([128, 2 * G, S]), ALU.mult)\
                    .then_inc(soft_n, 1)

            def reduce_piece(b, p):
                unit = b * PIECES + p
                ve.wait_ge(mx_done, due(mx_done, unit + 1))
                ve.tensor_reduce(mx_p[:, p:p + 1], mx_ps[unit % 2][:, 0:KP], AX.X, ALU.max).then_inc(red_done, 1)
                if p == PIECES - 1:
                    negated_maxima(b)

            def negated_maxima(b):
                ve.wait_ge(red_done, due(red_done, (b + 1) * PIECES))
                ve.tensor_reduce(nm[:, :], mx_p[:, :].rearrange("p (j k) -> p j k", k=3), AX.X, ALU.max, negate=True)\
                    .then_inc(nm_step, 1)
                ve.wait_ge(nm_step, due(nm_step, 3 * b + 1))
                if b:
                    ve.wait_ge(ps["MT"], due(ps["MT"], b))
                ve.tensor_copy(nm_hl[:, 0, :], nm[:, :]).then_inc(nm_step, 1)
                ve.wait_ge(nm_step, due(nm_step, 3 * b + 2))
                ve.tensor_tensor(nm_hl[:, 1, :], nm[:, :], nm_hl[:, 0, :].bitcast(F32), ALU.subtract)\
                    .then_inc(nm_step, 1)

            ve.memset(x_sb[:, :, :], 0.0).then_inc(dve_c, 1)
            ve.memset(vhat[:, :, :, :], 0.0)
            ve.memset(eps_col[:, :], EPS)
            ve.memset(minus_half[:, :], -0.5).then_inc(dve_c, 1)
            step("L0", 0)
            step("N0", 0)
            ve.wait_ge(pool_c, due(pool_c, IDENT_MADE))
            ve.tensor_reduce(gmask[:, :], ident[:, :].rearrange("p (g d) -> p g d", d=HD), AX.X, ALU.add)
            ve.tensor_reduce(e8[:, :], ident[:, :].rearrange("p (a e) -> p e a", e=8), AX.X, ALU.add)\
                .then_inc(dve_c, 1)
            ve.wait_ge(dve_c, due(dve_c, 3))
            step("K", 0)
            step("A", 0)
            ve.wait_ge(pool_c, due(pool_c, MASKS_MADE))
            for name in ("S0", "S1", "S2", "S3"):
                step(name, 0)
            ve.wait_ge(raw_in, due(raw_in, 16 * 3))
            ve.tensor_tensor(gkron[:, :, :], g8[:, :].unsqueeze(2).to_broadcast([128, PAIRS, 8]),
                             e8[:, :].unsqueeze(1).to_broadcast([128, PAIRS, 8]), ALU.mult).then_inc(dve_c, 1)
            step("SN0", 0)
            step("SN1", 0)
            for name in ("W1", "N1", "H0", "H1", "H2", "H3"):
                step(name, 0)

            def body(i):
                for g in range(2 * GROUPS):
                    part, gg = g // GROUPS, g % GROUPS
                    bm = 2 * i + part
                    if bm < B:
                        for p in pieces_within(g):
                            reduce_piece(bm, p)
                    for name, n in steps_of(i, g):
                        step(name, n, i, g)

            run_bodies(ve, at, body)

        @block.gpsimd
        def _(po):
            at = [None]
            due = counter(at)

            def add_up(b, half):
                if 0 <= b < B:
                    base = (b * 2 + half) * ADDS
                    dst = acc[:, b // 2 % 2, half * 8:(half + 1) * 8, b % 2 * SLOT:b % 2 * SLOT + S]
                for k in range(1, ADDS + 1):
                    if 0 <= b < B:
                        unit = (b * 2 + half) * 12 + k
                        po.wait_ge(exp_done, due(exp_done, unit + 1))
                        if k == 1:
                            first = p_ring[:, (unit - 1) % PR, :].rearrange("p (h s) -> p h s", s=S)
                        else:
                            po.wait_ge(acc_done, due(acc_done, base + k - 1))
                            first = dst
                        po.tensor_tensor(dst, first, p_ring[:, unit % PR, :].rearrange("p (h s) -> p h s", s=S), ALU.add).then_inc(acc_done, 1)

            def power(which, n):
                if not 0 <= n < PAIRS:
                    return
                po.wait_ge(ln[which], due(ln[which], (3 * n + 2, 4 * n + 3, 5 * n + 4)[which]))
                po.tensor_tensor(rstd[:, which, 0:1], mv[:, which, 1:2], eps_col[:, :], ALU.add)\
                    .then_inc(ln_eps[which], 1)
                po.wait_ge(ln_eps[which], due(ln_eps[which], n + 1))
                po.tensor_tensor(rstd[:, which, 1:2], rstd[:, which, 0:1], minus_half[:, :], ALU.pow)\
                    .then_inc(ln_pow[which], 1)

            made = [0]

            def make(instruction):
                made[0] += 1
                instruction.then_inc(pool_c, 1)
                po.wait_ge(pool_c, due(pool_c, made[0]))

            make(po.memset(ident[:, :], 0.0))
            make(po.affine_select(out=ident[:, :], in_=ident[:, :], compare_op=ALU.not_equal, fill=1.0,
                                  base=0, pattern=[[-1, 128]], channel_multiplier=1))
            assert made[0] == IDENT_MADE
            po.wait_ge(dve_c, due(dve_c, 2))
            power(0, 0)
            make(po.memset(cmask[:, :], 0.0))
            for h in range(2):
                half_mask = cmask[h * SLOT:(h + 1) * SLOT, :]
                make(po.affine_select(out=half_mask, in_=half_mask, compare_op=ALU.is_ge, fill=NEG, base=0,
                                      pattern=[[-1, S]], channel_multiplier=1))
            make(po.memset(p1[:, :, S:SLOT], 0.0))
            assert made[0] == MASKS_MADE
            make(po.memset(ones[:, :], 1.0))

            make(po.memset(y_t[:, :, :], 0.0))
            make(po.memset(cqt[64:96, :], 0.0))
            make(po.memset(wqk_sb[64:96, :, :, :], 0.0))
            make(po.memset(ax_t[64:96, :], 1.0))
            make(po.memset(b_sb[64:96, :], 0.0))
            assert made[0] == PADS_MADE
            make(po.memset(c_st[96:98, :, :].bitcast(F32), 1.0))
            po.wait_ge(eff_out, due(eff_out, 32))
            make(po.memset(acc[:, :, :, :], 1.0))
            assert made[0] == ALL_MADE
            power(1, 0)

            def body(i):
                power(0, i + 1)
                for half in range(2):
                    add_up(2 * i - 1, half)
                add_up(2 * i, 0)
                power(1, i + 1)
                power(2, i - 1)
                add_up(2 * i, 1)

            run_bodies(po, at, body)


def kernel(**inputs):
    import numpy as np
    import concourse.bacc as bacc
    from concourse.bass_utils import run_bass_kernel_spmd

    a = {k: np.asarray(v) for k, v in inputs.items()}
    arrays = {
        "x": a["x"].reshape(PAIRS, 2, S, D),
        "ctx_t": a["ctx_4096"].transpose(0, 2, 1),
        "wq": a["L0_attn_wq"].reshape(D, G, R, HD).transpose(0, 2, 1, 3).reshape(D, D),
        "wk": a["L0_attn_wk"],
        "wv": a["L0_attn_wv"],
        "wo": a["L0_attn_wo"].reshape(G, R, HD, D).transpose(1, 0, 2, 3).reshape(D, D),
        "wq_d": a["L0_xattn_Wq_d"],
        "w_qk": a["L0_xattn_W_qk"],
        "wkv_d": a["L0_xattn_Wkv_d"],
        "wv_u": a["L0_xattn_Wv_u"],
        "gate_t": np.repeat(a["L0_ffn_gate"].transpose(1, 0), 8, axis=0),
        "kern": a["L0_ffn_kernel"],
        "bias": a["L0_ffn_bias"].reshape(1, D),
        "lora_a": a["L0_ffn_lora_A"].transpose(0, 2, 1),
        "lora_b": a["L0_ffn_lora_B"].transpose(0, 2, 1),
        "lora_as": a["L0_ffn_lora_A_shared"].transpose(1, 0),
        "lora_bs": a["L0_ffn_lora_B_shared"].transpose(1, 0),
    }
    nc = bacc.Bacc("TRN2", target_bir_lowering=False, num_devices=1, dynamic_dma_scratch_size=1024)
    ins, feed = {}, {}
    for name, value in arrays.items():
        value = np.ascontiguousarray(value)
        feed[f"in_{name}"] = value
        ins[name] = nc.dram_tensor(f"in_{name}", value.shape, mybir.dt.from_np(value.dtype), kind="ExternalInput").ap()
    out = nc.dram_tensor("out_y", (PAIRS, 2, S, D), F32, kind="ExternalOutput").ap()
    decoder_layer(nc, **ins, out=out)
    result = run_bass_kernel_spmd(nc, [feed], core_ids=[0])
    return result.results[0]["out_y"].reshape(B, S, D)
```

```python
from contextlib import ExitStack

import concourse.bass as bass
from concourse import mybir

F32 = mybir.dt.float32
F32R = mybir.dt.float32r
ALU = mybir.AluOpType
ACT = mybir.ActivationFunctionType
AX = mybir.AxisListType

B, S, D = 16, 56, 512
PAIRS = B // 2
SLOT = 64
CH = D // 128
G, R, HD = 8, 4, 16
H, L = 16, 32
LQ = D // 8
NK = 1500
KT = NK // 4
KC = 125
KG = KT // KC
HN = H * S
HALF = HN // 2
ROWT = HN // 128
KP = NK // 3
PIECES = ROWT * 3
RANK, NL = 32, 16
EPS = 1e-5
NEG = -1e30
PR = 8
STB = 2
MXB = 3
GROUPS = 2 * KG
ADDS = 4 * KG - 1
LOOP_BODIES = 2
FIRST_LOOPED, LAST_LOOPED = 1, 6
IDENT_MADE, MASKS_MADE, PADS_MADE, ALL_MADE = 2, 6, 10, 12

PIECES_IN = [3, 2, 4, 3, 0, 0, 0, 3, 4, 1, 3, 0]
STEPS = [
    [("Ah", "a"), ("M", 2), ("L0", "n"), ("M", 1), ("A", "a"), ("AS", "a"), ("N0", "n")],
    [("CT", "a"), ("M", 1), ("T1", "n")],
    [("K", "n"), ("M", 1), ("Qh", "n"), ("M", 3), ("Q1", "n")],
    [("M", 1), ("S0", "n"), ("S1", "n"), ("S2", "n"), ("S3", "n"), ("SM0", "n"), ("NM", "m"), ("SM1", "n")],
    [("SE0", "n"), ("Ah", "b"), ("MT", "m"), ("A", "b"), ("SE1", "n"), ("V", "n"), ("SN0", "n")],
    [("CT", "b"), ("AS", "b"), ("SN1", "n")],
    [("P0", "n"), ("M", 1), ("P1", "n"), ("M", 1), ("P2", "n"), ("P3", "n"), ("XC", "f"), ("M", 1)],
    [("O1", "n"), ("M", 3), ("Y", "f")],
    [("DN", "f"), ("Wh", "n"), ("M", 1), ("W1", "n"), ("M", 1), ("DT", "f"), ("N1", "n")],
    [("YT", "f"), ("T2", "n"), ("M", 2), ("CQ", "n"), ("H0", "n"), ("N2", "f")],
    [("H1", "n"), ("NM", "o"), ("T3", "f")],
    [("MT", "o"), ("F1", "f"), ("Fh", "f"), ("H2", "n"), ("F2", "f"), ("H3", "n")],
]
BANK = {"Ah": (1, 0), "A": (1, 0), "CT": (1, 0), "MT": (0, 1), "T1": 1, "K": 1, "Qh": 0, "Q1": 0,
        "S0": 1, "S1": 0, "S2": 1, "S3": 0, "V": 0, "P0": 1, "P1": 0, "P2": 1, "P3": 0, "O1": 0, "Y": 1,
        "DN": 1, "Wh": 0, "W1": 0, "DT": 1, "YT": 1, "T2": 0, "CQ": 0, "H0": 1, "H1": 1, "T3": 0,
        "F1": 0, "H2": 0, "Fh": 1, "F2": 1, "H3": 0}


def steps_of(i, g):
    done = sum(PIECES_IN[g // GROUPS * GROUPS:g + 1])
    done += sum(w for h in range(g // GROUPS * GROUPS, g) for name, w in STEPS[h] if name == "M")
    for name, w in STEPS[g]:
        if name == "M":
            if 2 * i + g // GROUPS < B:
                yield name, range(done, done + w)
            done += w
            continue
        n = {"n": i + 1, "f": i - 1, "a": 2 * i + 1, "b": 2 * i + 2, "m": 2 * i, "o": 2 * i + 1}[w]
        if 0 <= n < (PAIRS if w in "nf" else B):
            yield name, n


def pieces_within(g):
    done = sum(PIECES_IN[g // GROUPS * GROUPS:g])
    done += sum(w for h in range(g // GROUPS * GROUPS, g) for name, w in STEPS[h] if name == "M")
    return range(done, done + PIECES_IN[g])


def decoder_layer(nc, x, ctx_t, wq, wk, wv, wo, wq_d, w_qk, wkv_d, wv_u, gate_t, kern, bias,
                  lora_a, lora_b, lora_as, lora_bs, out):
    with ExitStack() as stack:
        rates = {}

        def sb(name, shape, dt=F32):
            return stack.enter_context(nc.sbuf_tensor(name, shape, dt))

        def bank(name):
            return stack.enter_context(nc.psum_tensor(name, [128, 512], F32))

        def sem(name, per_pair):
            s = stack.enter_context(nc.semaphore(name))
            rates[s.name] = per_pair * LOOP_BODIES
            return s

        ctx_sb = sb("ctx_sb", [128, 2, CH, NK])
        wq_sb = sb("wq_sb", [128, CH, D])
        wk_sb = sb("wk_sb", [128, CH, 128])
        wv_sb = sb("wv_sb", [128, CH, 128])
        wo_sb = sb("wo_sb", [128, R, D])
        wqd_sb = sb("wqd_sb", [128, CH, LQ])
        wkv_sb = sb("wkv_sb", [128, CH, L])
        wqk_sb = sb("wqk_sb", [128, H, 3, L])
        wvu_sb = sb("wvu_sb", [128, D])
        kern_sb = sb("kern_sb", [128, CH, D])
        a_sb = sb("a_sb", [128, CH, 2 * RANK])
        b_sb = sb("b_sb", [96, D])
        c_st = sb("c_st", [98, 4, NK], F32R)
        c_nat = sb("c_nat", [KC, 4, KG, 128])
        q_st = sb("q_st", [98, 2, 2, HN], F32R)
        p_ring = sb("p_ring", [KC, PR, HALF])
        acc = sb("acc", [KC, 2, H, 128])
        ox = sb("ox", [128, H, 2, S])
        p1 = sb("p1", [128, R * G, SLOT])
        p1t = sb("p1t", [128, G // 2, R, 128])
        x_sb = sb("x_sb", [128, 2, D])
        x2_sb = sb("x2_sb", [128, 2, D])
        xn = sb("xn", [128, D])
        x3 = sb("x3", [128, D])
        x3n = sb("x3n", [128, D])
        xnt = sb("xnt", [128, CH, 128])
        qt = sb("qt", [128, R, 128])
        khat = sb("khat", [128, 2, G, S])
        vhat = sb("vhat", [128, 2, G // 2, 2 * HD])
        cqt = sb("cqt", [128, 128])
        ct_f = sb("ct_f", [128, KT])
        ct_hl = sb("ct_hl", [128, 2, KT], F32R)
        mx_p = sb("mx_p", [128, PIECES])
        nm = sb("nm", [128, ROWT])
        nm_hl = sb("nm_hl", [128, 2, ROWT], F32R)
        m_t = sb("m_t", [2 * ROWT, 128])
        den = sb("den", [128, 512])
        r_den = sb("r_den", [128, H])
        y_t = sb("y_t", [128, H // 4, 128])
        ax_t = sb("ax_t", [96, 128])
        sm = sb("sm", [128, 3, R * G])
        stats = sb("stats", [128, 3, 7])
        mv = sb("mv", [128, 3, 2])
        rstd = sb("rstd", [128, 3, 2])
        ident = sb("ident", [128, 128])
        ones = sb("ones", [128, L])
        gmask = sb("gmask", [128, G])
        e8 = sb("e8", [128, 8])
        cmask = sb("cmask", [128, S])
        minus_half = sb("minus_half", [128, 1])
        eps_col = sb("eps_col", [128, 1])
        g8 = sb("g8", [128, PAIRS])
        gkron = sb("gkron", [128, PAIRS, 8])
        spare = ctx_sb[:, 1, :, :].rearrange("p c k -> p (c k)")
        lora_raw = [spare[:, 0:2048], spare[:, 2048:4096]]
        lora_eff = [p_ring[0:64, :, :].rearrange("p a b -> p (a b)"),
                    acc[0:64, :, :, :].rearrange("p a h s -> p (a h s)")]

        st_ps = [bank(f"st_ps{n}") for n in range(STB)]
        mx_ps = [bank(f"mx_ps{n}") for n in range(MXB)]
        pv_ps = bank("pv_ps")
        mi_ps = [bank(f"mi_ps{n}") for n in range(2)]

        a_eff = nc.dram_tensor("a_eff", [PAIRS, D, RANK], F32).ap()
        b_eff = nc.dram_tensor("b_eff", [PAIRS, RANK, D], F32).ap()

        x_in = [sem(f"x_in{n}", 16) for n in range(2)]
        ctx_in = [sem(f"ctx_in{n}", 16) for n in range(2)]
        ab_in = sem("ab_in", 32)
        for s in x_in + ctx_in:
            rates[s.name] = 32
        w_attn = sem("w_attn", 0)
        w_out = sem("w_out", 0)
        w_latent = sem("w_latent", 0)
        w_cross = sem("w_cross", 0)
        w_ffn = sem("w_ffn", 0)
        raw_in = sem("raw_in", 0)
        eff_out = sem("eff_out", 0)
        cst_in = [sem(f"cst_in{n}", 0) for n in range(4)]
        for s in cst_in:
            rates[s.name] = 16 * 12
        m_in = [sem(f"m_in{n}", 32) for n in range(2)]
        y_out = sem("y_out", 32)
        pool_c = sem("pool_c", 0)
        dve_c = sem("dve_c", 0)
        lora_ps = sem("lora_ps", 0)
        lora_sb = sem("lora_sb", 0)
        ln = [sem("ln0", 3), sem("ln1", 4), sem("ln2", 5)]
        ln_eps = [sem(f"ln_eps{n}", 1) for n in range(3)]
        x3_base = sem("x3_base", 1)
        ln_pow = [sem(f"ln_pow{n}", 1) for n in range(3)]
        st_done = sem("st_done", 48)
        exp_done = sem("exp_done", 48)
        pv_done = sem("pv_done", 12)
        ox_sb = sem("ox_sb", 4)
        acc_done = sem("acc_done", 4 * ADDS)
        mx_done = sem("mx_done", 2 * PIECES)
        red_done = sem("red_done", 2 * PIECES)
        nm_step = sem("nm_step", 2 * 3)
        ps = {}
        for name in BANK:
            if name[-1] == "h":
                continue
            ps[name] = sem("ps_" + name, 2 if name in ("A", "CT", "MT") else 1)
        t1_sb = sem("t1_sb", 1)
        k_sb = sem("k_sb", 2)
        v_sb = sem("v_sb", 4)
        q1_sb = sem("q1_sb", 1)
        s1_sb = sem("s1_sb", 4)
        soft = sem("soft", 4)
        soft_e = sem("soft_e", 2)
        soft_n = sem("soft_n", 6)
        pt_sb = sem("pt_sb", 4)
        o1_sb = sem("o1_sb", 1)
        t2_sb = sem("t2_sb", 1)
        cq_sb = sem("cq_sb", 1)
        qh_hi = sem("qh_hi", 4)
        qh_lo = sem("qh_lo", 4)
        a_f = sem("a_f", 2)
        a_hi = sem("a_hi", 2)
        a_lo = sem("a_lo", 2)
        ct_sb = sem("ct_sb", 2)
        mt_sb = sem("mt_sb", 2)
        yu_sb = sem("yu_sb", 1)
        dn_sb = sem("dn_sb", 1)
        r_sb = sem("r_sb", 1)
        t3_sb = sem("t3_sb", 1)
        f1_sb = sem("f1_sb", 1)
        f2_sb = sem("f2_sb", 1)

        def step_bank(name, n):
            b = BANK[name]
            return mi_ps[b[n % 2] if isinstance(b, tuple) else b]

        def lora_bank(q):
            return [*st_ps, *mx_ps, pv_ps][q % 6]

        block = stack.enter_context(nc.Block())

        def counter(at):
            def due(s, count):
                assert count > 0
                return count if at[0] is None else at[0] * rates[s.name] + count
            return due

        def run_bodies(eng, at, body):
            body(0)
            with eng.Fori(0, (LAST_LOOPED - FIRST_LOOPED + 1) // LOOP_BODIES) as rnd:
                at[0] = rnd
                for i in range(FIRST_LOOPED, FIRST_LOOPED + LOOP_BODIES):
                    body(i)
                at[0] = None
            for i in range(LAST_LOOPED + 1, PAIRS + 1):
                body(i)

        @block.sync
        def _(sp):
            at = [None]
            due = counter(at)
            dma = sp.dma_start

            def pair_index(n):
                return n if at[0] is None else at[0] * LOOP_BODIES + n

            def batch_index(b):
                return b if at[0] is None else at[0] * (2 * LOOP_BODIES) + b

            def load_x(n):
                if n >= 2:
                    sp.wait_ge(ln[1], due(ln[1], 4 * (n - 2) + 1))
                for h in range(2):
                    dma(x_sb[h * SLOT:h * SLOT + S, n % 2, :], x[pair_index(n), h]).then_inc(x_in[n % 2], 16)

            def load_ctx(b):
                if b >= 2:
                    sp.wait_ge(ps["A"], due(ps["A"], b - 1))
                dma(ctx_sb[:, b % 2, :, :],
                    ctx_t[batch_index(b)].rearrange("(p c) k -> p c k", c=CH)).then_inc(ctx_in[b % 2], 16)

            def load_ab(n):
                dma(a_sb[:, :, 0:RANK],
                    a_eff[pair_index(n)].rearrange("(c p) r -> p c r", p=128)).then_inc(ab_in, 16)
                dma(b_sb[0:RANK, :], b_eff[pair_index(n)]).then_inc(ab_in, 16)

            def spread_ct(b):
                for part, dst in ((0, 0), (1, L), (0, 2 * L)):
                    if dst == 0:
                        sp.wait_ge(a_hi, due(a_hi, b + 1))
                    if dst == L:
                        sp.wait_ge(a_lo, due(a_lo, b + 1))
                    for t in range(4):
                        dma(c_st[dst:dst + L, b % 4, t * KT:(t + 1) * KT].bitcast(F32),
                            ct_hl[t * L:(t + 1) * L, part, :].bitcast(F32)).then_inc(cst_in[b % 4], 16)

            def spread_m(b):
                sp.wait_ge(mt_sb, due(mt_sb, b + 1))
                for part in range(2):
                    dma(q_st[96 + part:97 + part, b // 2 % 2, b % 2, :].bitcast(F32)
                        .rearrange("a (j p) -> a j p", p=128),
                        m_t[part * ROWT:(part + 1) * ROWT, :]).then_inc(m_in[b % 2], 16)

            def store_y(n):
                sp.wait_ge(f2_sb, due(f2_sb, n + 1))
                for h in range(2):
                    dma(out[pair_index(n), h], x3n[h * SLOT:h * SLOT + S, :]).then_inc(y_out, 16)

            sp.wait_ge(dve_c, due(dve_c, 1))
            load_x(0)
            for c in range(2):
                dma(wq_sb[:, 2 * c:2 * c + 2, :], wq[c * 256:(c + 1) * 256, :].rearrange("(c p) n -> p c n", p=128))\
                    .then_inc(w_attn, 16)
            dma(wk_sb[:, :, :], wk.rearrange("(c p) n -> p c n", p=128)).then_inc(w_attn, 16)
            dma(wv_sb[:, :, :], wv.rearrange("(c p) n -> p c n", p=128)).then_inc(w_attn, 16)
            dma(wkv_sb[:, :, :], wkv_d.rearrange("(p c) n -> p c n", c=CH)).then_inc(w_latent, 16)
            for k in range(2):
                dma(lora_raw[k], (lora_a, lora_b)[k].rearrange("n (e f) r -> (n e) (f r)", e=8)).then_inc(raw_in, 16)
            dma(g8[:, :], gate_t).then_inc(raw_in, 16)
            load_ctx(0)
            dma(wo_sb[:, :, :], wo.rearrange("(r p) n -> p r n", p=128)).then_inc(w_out, 16)
            dma(wqd_sb[:, :, :], wq_d.rearrange("(c p) n -> p c n", p=128)).then_inc(w_cross, 16)
            for k in range(3):
                for half in range(2):
                    dma(wqk_sb[half * LQ:(half + 1) * LQ, :, k, :], w_qk.rearrange("p (h l) -> p h l", l=L))\
                        .then_inc(w_cross, 16)
            for t in range(4):
                dma(wvu_sb[t * L:(t + 1) * L, :], wv_u).then_inc(w_cross, 16)
            spread_ct(0)
            sp.wait_ge(lora_ps, due(lora_ps, 8))
            load_ctx(1)
            dma(kern_sb[:, :, :], kern.rearrange("(c p) n -> p c n", p=128)).then_inc(w_ffn, 16)
            sp.wait_ge(pool_c, due(pool_c, PADS_MADE))
            dma(a_sb[:, :, RANK:2 * RANK], lora_as.rearrange("(c p) r -> p c r", p=128)).then_inc(w_ffn, 16)
            dma(b_sb[RANK:2 * RANK, :], lora_bs).then_inc(w_ffn, 16)
            dma(b_sb[2 * RANK:2 * RANK + 1, :], bias).then_inc(y_out, 16)
            sp.wait_ge(eff_out, due(eff_out, 32))

            def body(i):
                if 2 * i + 2 < B:
                    load_x(i + 1)
                    load_ctx(2 * i + 2)
                for g in range(2 * GROUPS):
                    for name, n in steps_of(i, g):
                        if name == "A":
                            spread_ct(n)
                            if n % 2 and n + 2 < B:
                                load_ctx(n + 2)
                        elif name == "MT":
                            spread_m(n)
                        elif name == "Y":
                            load_ab(n)
                        elif name == "F2":
                            store_y(n)

            run_bodies(sp, at, body)
            sp.wait_ge(y_out, due(y_out, 32 * PAIRS + 16))

        @block.tensor
        def _(pe):
            at = [None]
            due = counter(at)
            mm = pe.matmul

            def four_transposes(bank_, src):
                for c in range(4):
                    last = pe.transpose(bank_[:, c * 128:(c + 1) * 128], src[:, c * 128:(c + 1) * 128], ident[:, :])
                return last

            def queries(o, heads):
                for r in heads:
                    for c in range(CH):
                        last = mm(o[:, r * 128:(r + 1) * 128], wq_sb[:, c, r * 128:(r + 1) * 128],
                                  xnt[:, c, :], start=(c == 0), stop=(c == CH - 1))
                return last

            def latents(o, slot, chunks):
                for c in chunks:
                    for t in range(4):
                        last = mm(o[t * L:(t + 1) * L, 0:KT], wkv_sb[:, c, :],
                                  ctx_sb[:, slot, c, t * KT:(t + 1) * KT], start=(c == 0), stop=(c == CH - 1))
                return last

            def step(name, n, i=0, g=0):
                if name == "M":
                    for p in n:
                        maxima(2 * i + g // GROUPS, p)
                if name not in BANK:
                    return
                o = step_bank(name, n)
                slot = n % 2
                if name == "T1":
                    pe.wait_ge(ln[0], due(ln[0], 3 * n + 3))
                    last = four_transposes(o, xn)
                elif name == "K":
                    pe.wait_ge(t1_sb, due(t1_sb, n + 1))
                    for c in range(CH):
                        last = mm(o[:, 0:128], wk_sb[:, c, :], xnt[:, c, :], start=(c == 0), stop=(c == CH - 1))
                elif name == "V":
                    if n:
                        pe.wait_ge(mt_sb, due(mt_sb, 2 * n - 1))
                    for c in range(CH):
                        last = mm(o[:, 0:128], xnt[:, c, :], wv_sb[:, c, :], start=(c == 0), stop=(c == CH - 1))
                elif name == "Qh":
                    if n:
                        pe.wait_ge(ct_sb, due(ct_sb, 2 * n))
                    queries(o, (0, 1))
                    return
                elif name == "Q1":
                    last = queries(o, (2, 3))
                elif name in ("S0", "S1", "S2", "S3"):
                    r = int(name[1])
                    if r == 0:
                        pe.wait_ge(q1_sb, due(q1_sb, n + 1))
                        pe.wait_ge(k_sb, due(k_sb, 2 * n + 2))
                    if r >= 2:
                        pe.wait_ge(s1_sb, due(s1_sb, 4 * n + r - 1))
                    for b in range(2):
                        last = mm(o[b * SLOT:(b + 1) * SLOT, 0:G * S], qt[:, r, b * SLOT:(b + 1) * SLOT],
                                  khat[:, b, :, :].rearrange("p g k -> p (g k)"), start=True, stop=True)
                elif name in ("P0", "P1", "P2", "P3"):
                    r = int(name[1])
                    if r == 0:
                        pe.wait_ge(ct_sb, due(ct_sb, 2 * n + 1))
                    if r % 2 == 0:
                        pe.wait_ge(soft_n, due(soft_n, 6 * n + 3 * (r // 2) + 3))
                    if r == 1:
                        pe.wait_ge(v_sb, due(v_sb, 4 * n + 4))
                    if r >= 2:
                        pe.wait_ge(pt_sb, due(pt_sb, 4 * n + r - 1))
                    last = four_transposes(o, p1[:, r * G:(r + 1) * G, :].rearrange("p g k -> p (g k)"))
                elif name == "O1":
                    pe.wait_ge(pt_sb, due(pt_sb, 4 * n + 4))
                    for b in range(2):
                        for g in range(G // 2):
                            last = mm(o[g * 32:(g + 1) * 32, b * 256:(b + 1) * 256], vhat[:, b, g, :],
                                      p1t[:, g, :, b * SLOT:(b + 1) * SLOT], start=True, stop=True)
                elif name == "Wh":
                    pe.wait_ge(o1_sb, due(o1_sb, n + 1))
                    for r in range(R // 2):
                        mm(o[:, :], qt[:, r, :], wo_sb[:, r, :], start=(r == 0), stop=False)
                    return
                elif name == "W1":
                    for r in range(R // 2, R):
                        last = mm(o[:, :], qt[:, r, :], wo_sb[:, r, :], start=False, stop=(r == R - 1))
                elif name == "T2":
                    pe.wait_ge(ln[1], due(ln[1], 4 * n + 4))
                    last = four_transposes(o, xn)
                elif name == "CQ":
                    pe.wait_ge(t2_sb, due(t2_sb, n + 1))
                    for c in range(CH // 2):
                        for half in range(2):
                            k = half * (CH // 2) + c
                            last = mm(o[half * LQ:(half + 1) * LQ, 0:128], wqd_sb[:, k, :], xnt[:, k, :],
                                      start=(c == 0), stop=(c == CH // 2 - 1))
                elif name in ("H0", "H1", "H2", "H3"):
                    k = int(name[1])
                    if k == 0:
                        pe.wait_ge(cq_sb, due(cq_sb, n + 1))
                    if k == 0 and n >= 2:
                        pe.wait_ge(ln[2], due(ln[2], 5 * n - 9))
                    if k == 1:
                        pe.wait_ge(qh_lo, due(qh_lo, 4 * n + 1))
                    if k == 2 and n >= 2:
                        pe.wait_ge(f1_sb, due(f1_sb, n - 1))
                    if k == 3:
                        pe.wait_ge(qh_lo, due(qh_lo, 4 * n + 3))
                    for h in range(4):
                        head = 4 * k + h
                        last = mm(o[0:96, h * 2 * S:(h + 1) * 2 * S], wqk_sb[:, head, :, :].rearrange("p k l -> p (k l)"),
                                  cqt[:, :].rearrange("p (b s) -> p b s", b=2)[:, :, 0:S], start=True, stop=True)
                elif name == "Ah":
                    if n % 2:
                        pe.wait_ge(qh_lo, due(qh_lo, 2 * n + 2))
                    elif n:
                        pe.wait_ge(s1_sb, due(s1_sb, 2 * n + 3))
                    pe.wait_ge(ctx_in[slot], due(ctx_in[slot], 16 * (n // 2 + 1)))
                    latents(o, slot, (0, 1))
                    return
                elif name == "A":
                    last = latents(o, slot, (2, 3))
                elif name == "CT":
                    pe.wait_ge(a_f, due(a_f, n + 1))
                    for k in range(KG):
                        last = pe.transpose(o[0:KC, k * 128:(k + 1) * 128], ct_f[:, k * KC:(k + 1) * KC], ident[:, :])
                elif name == "MT":
                    if n % 2 == 0 and n + 2 < B:
                        pe.wait_ge(s1_sb, due(s1_sb, 2 * n + 8))
                    if n == B - 2:
                        pe.wait_ge(ct_sb, due(ct_sb, B))
                    if n % 2 and n + 1 < B:
                        pe.wait_ge(qh_lo, due(qh_lo, 2 * n + 4))
                    pe.wait_ge(nm_step, due(nm_step, 3 * n + 3))
                    last = pe.transpose(o[0:2 * ROWT, 0:128],
                                        nm_hl[:, :, :].rearrange("p a j -> p (a j)").bitcast(F32), ident[:, :])
                elif name == "Y":
                    if n + 2 >= PAIRS:
                        pe.wait_ge(f2_sb, due(f2_sb, n))
                    pe.wait_ge(ox_sb, due(ox_sb, 4 * n + 4))
                    for h in range(H):
                        t, q = h % 4, h // 4
                        last = mm(o[t * 32:(t + 1) * 32, q * 2 * S:(q + 1) * 2 * S], wvu_sb[:, h * L:(h + 1) * L],
                                  ox[:, h, :, :].rearrange("p b s -> p (b s)"), start=True, stop=True)
                elif name == "DN":
                    pe.wait_ge(yu_sb, due(yu_sb, n + 1))
                    pe.wait_ge(acc_done, due(acc_done, 4 * ADDS * (n + 1)))
                    for t in range(4):
                        last = mm(o[t * L:(t + 1) * L, :], ones[0:KC, :], acc[:, slot, t:H:4, :], start=True, stop=True)
                elif name == "DT":
                    pe.wait_ge(dn_sb, due(dn_sb, n + 1))
                    last = four_transposes(o, den)
                elif name == "YT":
                    pe.wait_ge(r_sb, due(r_sb, n + 1))
                    pe.wait_ge(yu_sb, due(yu_sb, n + 1))
                    last = four_transposes(o, y_t[:, :, :].rearrange("p q s -> p (q s)"))
                elif name == "T3":
                    if n + 2 == PAIRS:
                        pe.wait_ge(mt_sb, due(mt_sb, B - 1))
                    pe.wait_ge(ln[2], due(ln[2], 5 * n + 5))
                    last = four_transposes(o, x3n)
                elif name == "F1":
                    pe.wait_ge(t3_sb, due(t3_sb, n + 1))
                    pe.wait_ge(ab_in, due(ab_in, 32 * (n + 1)))
                    for c in range(CH):
                        last = mm(o[0:2 * RANK, 0:128], a_sb[:, c, :], xnt[:, c, :],
                                  start=(c == 0), stop=(c == CH - 1))
                elif name == "Fh":
                    if 2 * n + 3 < B:
                        pe.wait_ge(mt_sb, due(mt_sb, 2 * n + 4))
                    for c in range(CH // 2):
                        mm(o[:, :], xnt[:, c, :], kern_sb[:, c, :], start=(c == 0), stop=False)
                    return
                elif name == "F2":
                    for c in range(CH // 2, CH):
                        mm(o[:, :], xnt[:, c, :], kern_sb[:, c, :], start=False, stop=False)
                    pe.wait_ge(f1_sb, due(f1_sb, n + 1))
                    last = mm(o[:, :], ax_t[:, :], b_sb[:, :], start=False, stop=True)
                last.then_inc(ps[name], 1)

            def scores(b, g, t):
                unit = b * 24 + g * 4 + t
                half, k = g // KG, g % KG
                if g == 0 and t == 0:
                    pe.wait_ge(m_in[b % 2], due(m_in[b % 2], 32 * (b // 2 + 1)))
                if unit >= STB:
                    pe.wait_ge(exp_done, due(exp_done, unit - STB + 1))
                mm(st_ps[unit % STB][0:KC, 0:HALF], c_st[:, b % 4, t * KT + k * KC:t * KT + (k + 1) * KC],
                   q_st[:, b // 2 % 2, b % 2, half * HALF:(half + 1) * HALF],
                   start=True, stop=True).then_inc(st_done, 1)

            def sums(b, g):
                half, k = g // KG, g % KG
                pe.wait_ge(exp_done, due(exp_done, b * 24 + g * 4 + 4))
                if g == 0:
                    pe.wait_ge(ct_sb, due(ct_sb, b + 1))
                if k == 0 and b * 2 + half:
                    pe.wait_ge(ox_sb, due(ox_sb, b * 2 + half))
                for t in range(4):
                    unit = b * 24 + g * 4 + t
                    last = mm(pv_ps[t * L:(t + 1) * L, 0:HALF], c_nat[:, b % 4, k, t * L:(t + 1) * L],
                              p_ring[:, unit % PR, :], start=(k == 0), stop=(k == KG - 1))
                last.then_inc(pv_done, 1)

            def maxima(b, p):
                j, k = p // 3, p % 3
                if p == 0:
                    pe.wait_ge(cst_in[b % 4], due(cst_in[b % 4], 16 * 12 * (b // 4 + 1)))
                if k == 0:
                    pe.wait_ge(qh_lo, due(qh_lo, 4 * (b // 2) + ((j + 1) * 128 - 1) // (4 * S) + 1))
                if b * PIECES + p >= MXB:
                    pe.wait_ge(red_done, due(red_done, b * PIECES + p - MXB + 1))
                mm(mx_ps[(b * PIECES + p) % MXB][:, 0:KP], q_st[0:96, b // 2 % 2, b % 2, j * 128:(j + 1) * 128],
                   c_st[0:96, b % 4, k * KP:(k + 1) * KP], start=True, stop=True).then_inc(mx_done, 1)

            def lora_factors(since, until):
                pe.wait_ge(raw_in, due(raw_in, 16 * 3))
                pe.wait_ge(dve_c, due(dve_c, 4))
                for q in range(since, until):
                    if q >= 6:
                        pe.wait_ge(lora_sb, due(lora_sb, q - 5))
                    mm(lora_bank(q)[0:64, :], gkron[:, :, :].rearrange("p i e -> p (i e)"),
                       lora_raw[q // 4][:, q % 4 * 512:(q % 4 + 1) * 512], start=True, stop=True)\
                        .then_inc(lora_ps, 1)

            pe.wait_ge(pool_c, due(pool_c, IDENT_MADE))
            step("T1", 0)
            pe.wait_ge(w_attn, due(w_attn, 16 * 4))
            for name in ("K", "Qh", "Q1", "S0", "S1", "S2", "S3"):
                step(name, 0)
            pe.wait_ge(s1_sb, due(s1_sb, 4))
            pe.wait_ge(w_latent, due(w_latent, 16))
            for name in ("Ah", "A", "V", "CT"):
                step(name, 0)
            lora_factors(0, 6)
            for name in ("P0", "P1", "P2", "P3", "O1"):
                step(name, 0)
            lora_factors(6, 8)
            pe.wait_ge(w_out, due(w_out, 16))
            step("Wh", 0)
            step("W1", 0)
            step("T2", 0)
            pe.wait_ge(w_cross, due(w_cross, 16 * 11))
            pe.wait_ge(pool_c, due(pool_c, PADS_MADE))
            for name in ("CQ", "H0", "H1", "H2", "H3"):
                step(name, 0)
            pe.wait_ge(w_ffn, due(w_ffn, 16 * 3))
            pe.wait_ge(y_out, due(y_out, 16))
            pe.wait_ge(lora_sb, due(lora_sb, 8))
            pe.wait_ge(pool_c, due(pool_c, ALL_MADE))

            def body(i):
                for g in range(2 * GROUPS):
                    part, gg = g // GROUPS, g % GROUPS
                    bs, bm = 2 * i - 1 + part, 2 * i + part
                    todo = pieces_within(g) if bm < B else []
                    bl, gl = (bs, gg - 1) if gg else (bs - 1, GROUPS - 1)
                    for t in range(4):
                        if 0 <= bs < B:
                            scores(bs, gg, t)
                        for p in todo[t:t + 1]:
                            maxima(bm, p)
                        if t == 1 and 0 <= bl < B:
                            sums(bl, gl)
                    for name, n in steps_of(i, g):
                        step(name, n, i, g)

            run_bodies(pe, at, body)

        @block.scalar
        def _(act):
            at = [None]
            due = counter(at)

            def copy(dst, src, scale=1.0):
                return act.activation(dst, src, ACT.Copy, scale=scale)

            def step(name, n, i=0, g=0):
                if name == "XC":
                    act.wait_ge(ln[1], due(ln[1], 4 * n + 4))
                    if n + 2 >= PAIRS:
                        act.wait_ge(f2_sb, due(f2_sb, n))
                    copy(x3[:, :], x2_sb[:, n % 2, :]).then_inc(x3_base, 1)
                    return
                if name not in ("T1", "V", "Q1", "P0", "P1", "P2", "P3", "SE0", "SE1", "O1", "T2", "CQ", "H0", "H1", "H2",
                                "H3", "A", "CT", "MT", "Y", "DN", "T3", "F1"):
                    return
                if name in ("SE0", "SE1"):
                    k = int(name[2])
                    rows = p1[:, k * 2 * G:(k + 1) * 2 * G, 0:S]
                    act.wait_ge(soft, due(soft, 4 * n + 2 * k + 2))
                    act.activation(rows, rows, ACT.Exp).then_inc(soft_e, 1)
                    return
                o = step_bank(name, n)
                act.wait_ge(ps[name], due(ps[name], n + 1))
                if name == "T1":
                    copy(xnt[:, :, :].rearrange("p c s -> p (c s)"), o[:, :]).then_inc(t1_sb, 1)
                elif name == "V":
                    for b in range(2):
                        for h in range(2):
                            src = o[b * SLOT:(b + 1) * SLOT, 0:128].rearrange("p (g e d) -> p g e d", g=4, e=2)
                            copy(vhat[h * 64:(h + 1) * 64, b, :, h * HD:(h + 1) * HD], src[:, :, h, :])\
                                .then_inc(v_sb, 1)
                elif name == "Q1":
                    copy(qt[:, :, :].rearrange("p r s -> p (r s)"), o[:, :], scale=float(HD) ** -0.5)\
                        .then_inc(q1_sb, 1)
                elif name[0] == "P":
                    copy(p1t[:, :, int(name[1]), :], o[:, :].rearrange("p (g s) -> p g s", g=4)).then_inc(pt_sb, 1)
                elif name == "O1":
                    copy(qt[:, :, :].rearrange("p r (b s) -> p b r s", b=2),
                         o[:, :].rearrange("p (b r s) -> p b r s", b=2, r=R)).then_inc(o1_sb, 1)
                elif name == "T2":
                    copy(xnt[:, :, :].rearrange("p c s -> p (c s)"), o[:, :]).then_inc(t2_sb, 1)
                elif name == "CQ":
                    copy(cqt[:, :], o[:, 0:128]).then_inc(cq_sb, 1)
                elif name[0] == "H":
                    k = int(name[1])
                    if n >= 2:
                        act.wait_ge(st_done, due(st_done, 24 * (2 * n - 2)))
                    for b in range(2):
                        last = copy(q_st[0:96, n % 2, b, k * 4 * S:(k + 1) * 4 * S].rearrange("p (h s) -> p h s", h=4),
                                    o[0:96, 0:448].rearrange("p (h b s) -> p b h s", b=2, s=S)[:, b])
                    last.then_inc(qh_hi, 1)
                elif name == "A":
                    if n:
                        act.wait_ge(a_lo, due(a_lo, n))
                    copy(ct_f[:, :], o[:, 0:KT]).then_inc(a_f, 1)
                elif name == "CT":
                    copy(c_nat[:, n % 4, :, :].rearrange("p k l -> p (k l)"), o[0:KC, 0:KG * 128])\
                        .then_inc(ct_sb, 1)
                elif name == "MT":
                    if n:
                        act.wait_ge(m_in[(n - 1) % 2], due(m_in[(n - 1) % 2], 32 * ((n - 1) // 2 + 1)))
                    copy(m_t[:, :], o[0:2 * ROWT, 0:128]).then_inc(mt_sb, 1)
                elif name == "Y":
                    copy(y_t[:, :, :].rearrange("p q (b s) -> p q b s", b=2)[:, :, :, 0:S],
                         o[:, 0:448].rearrange("p (q b s) -> p q b s", q=4, b=2)).then_inc(yu_sb, 1)
                elif name == "DN":
                    copy(den[:, :], o[:, :]).then_inc(dn_sb, 1)
                elif name == "T3":
                    copy(xnt[:, :, :].rearrange("p c s -> p (c s)"), o[:, :]).then_inc(t3_sb, 1)
                elif name == "F1":
                    copy(ax_t[0:2 * RANK, :], o[0:2 * RANK, 0:128]).then_inc(f1_sb, 1)

            def exponentials(b, g):
                half = g // KG
                for t in range(4):
                    unit = b * 24 + g * 4 + t
                    act.wait_ge(st_done, due(st_done, unit + 1))
                    old = unit - PR
                    if old >= 0:
                        act.wait_ge(pv_done, due(pv_done, old // 4 + 1))
                        act.wait_ge(acc_done, due(acc_done, old // 12 * ADDS + max(old % 12, 1)))
                    act.activation(p_ring[:, unit % PR, :], st_ps[unit % STB][0:KC, 0:HALF], ACT.Exp,
                                   scale=float(L) ** -0.5).then_inc(exp_done, 1)

            def out_of_sums(b, half):
                act.wait_ge(pv_done, due(pv_done, b * 6 + half * KG + KG))
                if b % 2 == 0 and half == 0 and b:
                    act.wait_ge(ps["Y"], due(ps["Y"], b // 2))
                copy(ox[:, half * 8:half * 8 + 8, b % 2, :],
                     pv_ps[:, 0:HALF].rearrange("p (h s) -> p h s", h=8)).then_inc(ox_sb, 1)

            act.wait_ge(dve_c, due(dve_c, 2))
            def lora_out(since, until):
                for q in range(since, until):
                    act.wait_ge(lora_ps, due(lora_ps, q + 1))
                    copy(lora_eff[q // 4][:, q % 4 * 512:(q % 4 + 1) * 512], lora_bank(q)[0:64, :])\
                        .then_inc(lora_sb, 1)

            for name in ("T1", "Q1", "SE0", "SE1", "A", "V", "CT"):
                step(name, 0)
            lora_out(0, 6)
            for name in ("P0", "P1", "P2", "P3", "O1"):
                step(name, 0)
            lora_out(6, 8)
            act.wait_ge(lora_sb, due(lora_sb, 8))
            for k, dst in enumerate((a_eff, b_eff)):
                act.dma_start(dst.rearrange("i (e f) r -> (i e) (f r)", e=8), lora_eff[k][:, 0:2048])\
                    .then_inc(eff_out, 16)
            for name in ("T2", "CQ", "H0", "H1", "H2", "H3"):
                step(name, 0)
            act.wait_ge(eff_out, due(eff_out, 32))

            def body(i):
                for g in range(2 * GROUPS):
                    part, gg = g // GROUPS, g % GROUPS
                    bs = 2 * i - 1 + part
                    if 0 <= bs < B:
                        exponentials(bs, gg)
                    bl, gl = (bs, gg - 1) if gg else (bs - 1, GROUPS - 1)
                    if 0 <= bl < B and gl % KG == KG - 1:
                        out_of_sums(bl, gl // KG)
                    for name, n in steps_of(i, g):
                        step(name, n, i, g)

            run_bodies(act, at, body)

        @block.vector
        def _(ve):
            at = [None]
            due = counter(at)

            def statistics(which, n, src):
                s = ln[which]
                k = (3 * n, 4 * n + 1, 5 * n + 2)[which]
                ve.bn_stats(stats[:, which, 0:6], src).then_inc(s, 1)
                ve.wait_ge(s, due(s, k + 1))
                ve.tensor_copy(stats[:, which, 6:7], eps_col[:, :])
                ve.bn_aggr(mv[:, which, :], stats[:, which, 0:6]).then_inc(s, 1)

            def normalise(which, n, src, dst):
                ve.wait_ge(ln_pow[which], due(ln_pow[which], n + 1))
                ve.tensor_scalar(dst, src, mv[:, which, 0:1], rstd[:, which, 1:2], ALU.subtract, ALU.mult)\
                    .then_inc(ln[which], 1)

            def step(name, n, i=0, g=0):
                if name == "M":
                    for p in n:
                        reduce_piece(2 * i + g // GROUPS, p)
                    return
                slot = n % 2
                if name == "L0":
                    ve.wait_ge(x_in[slot], due(x_in[slot], 32 * (n // 2 + 1)))
                    statistics(0, n, x_sb[:, slot, :])
                elif name == "N0":
                    normalise(0, n, x_sb[:, slot, :], xn[:, :])
                elif name == "N1":
                    normalise(1, n, x2_sb[:, slot, :], xn[:, :])
                elif name == "N2":
                    normalise(2, n, x3[:, :], x3n[:, :])
                elif name == "AS":
                    if n:
                        ve.wait_ge(cst_in[(n - 1) % 4], due(cst_in[(n - 1) % 4], 16 * 12 * ((n - 1) // 4 + 1)))
                    ve.wait_ge(a_f, due(a_f, n + 1))
                    ve.tensor_copy(ct_hl[:, 0, :], ct_f[:, :]).then_inc(a_hi, 1)
                    ve.wait_ge(a_hi, due(a_hi, n + 1))
                    ve.tensor_tensor(ct_hl[:, 1, :], ct_f[:, :], ct_hl[:, 0, :].bitcast(F32), ALU.subtract)\
                        .then_inc(a_lo, 1)
                elif name == "NM":
                    negated_maxima(n)
                elif name in ("SM0", "SM1"):
                    softmax(n, int(name[2]))
                elif name in ("SN0", "SN1"):
                    softmax_end(n, int(name[2]))
                if name not in BANK:
                    return
                o = step_bank(name, n)
                if name in ("K", "S0", "S1", "S2", "S3", "W1", "H0", "H1", "H2", "H3", "DT", "YT", "F2"):
                    ve.wait_ge(ps[name], due(ps[name], n + 1))
                if name == "K":
                    for b in range(2):
                        k = o[:, b * SLOT:b * SLOT + S].unsqueeze(1).to_broadcast([128, G, S])
                        ve.tensor_tensor(khat[:, b, :, :], k, gmask[:, :].unsqueeze(2).to_broadcast([128, G, S]),
                                         ALU.mult).then_inc(k_sb, 1)
                elif name in ("S0", "S1", "S2", "S3"):
                    r = int(name[1])
                    ve.tensor_tensor(p1[:, r * G:(r + 1) * G, 0:S], o[:, 0:G * S].rearrange("p (g k) -> p g k", g=G),
                                     cmask[:, :].unsqueeze(1).to_broadcast([128, G, S]), ALU.add)\
                        .then_inc(s1_sb, 1)
                elif name == "W1":
                    if n >= 2:
                        ve.wait_ge(x3_base, due(x3_base, n - 1))
                    ve.tensor_tensor(x2_sb[:, slot, :], o[:, :], x_sb[:, slot, :], ALU.add).then_inc(ln[1], 1)
                    ve.wait_ge(ln[1], due(ln[1], 4 * n + 1))
                    statistics(1, n, x2_sb[:, slot, :])
                elif name[0] == "H":
                    k = int(name[1])
                    ve.wait_ge(qh_hi, due(qh_hi, 4 * n + k + 1))
                    for b in range(2):
                        q = q_st[64:96, slot, b, k * 4 * S:(k + 1) * 4 * S].rearrange("p (h s) -> p h s", h=4)
                        last = ve.tensor_tensor(q, o[64:96, 0:448].rearrange("p (h b s) -> p b h s", b=2, s=S)[:, b],
                                                q.bitcast(F32), ALU.subtract)
                    last.then_inc(qh_lo, 1)
                elif name == "DT":
                    ve.reciprocal(r_den[:, :], o[:, 0:H * L:L]).then_inc(r_sb, 1)
                elif name == "YT":
                    ve.wait_ge(y_out, due(y_out, 32 * n + 16))
                    ve.wait_ge(r_sb, due(r_sb, n + 1))
                    ve.tensor_tensor(x3n[:, :].rearrange("p (h d) -> p h d", d=L),
                                     o[:, :].rearrange("p (h d) -> p h d", d=L),
                                     r_den[:, :].unsqueeze(2).to_broadcast([128, H, L]), ALU.mult).then_inc(ln[2], 1)
                    ve.wait_ge(ln[2], due(ln[2], 5 * n + 1))
                    ve.wait_ge(x3_base, due(x3_base, n + 1))
                    ve.tensor_tensor(x3[:, :], x3n[:, :], x3[:, :], ALU.add).then_inc(ln[2], 1)
                    ve.wait_ge(ln[2], due(ln[2], 5 * n + 2))
                    statistics(2, n, x3[:, :])
                elif name == "F2":
                    ve.tensor_tensor(x3n[:, :], o[:, :], x3[:, :], ALU.add).then_inc(f2_sb, 1)

            def softmax(n, k):
                rows = p1[:, k * 2 * G:(k + 1) * 2 * G, 0:S]
                most = sm[:, 0, k * 2 * G:(k + 1) * 2 * G]
                ve.wait_ge(s1_sb, due(s1_sb, 4 * n + 2 * k + 2))
                ve.tensor_reduce(most, rows, AX.X, ALU.max).then_inc(soft, 1)
                ve.wait_ge(soft, due(soft, 4 * n + 2 * k + 1))
                ve.tensor_tensor(rows, rows, most.unsqueeze(2).to_broadcast([128, 2 * G, S]), ALU.subtract)\
                    .then_inc(soft, 1)

            def softmax_end(n, k):
                rows = p1[:, k * 2 * G:(k + 1) * 2 * G, 0:S]
                total, inverse = (sm[:, j, k * 2 * G:(k + 1) * 2 * G] for j in (1, 2))
                ve.wait_ge(soft_e, due(soft_e, 2 * n + k + 1))
                ve.tensor_reduce(total, rows, AX.X, ALU.add).then_inc(soft_n, 1)
                ve.wait_ge(soft_n, due(soft_n, 6 * n + 3 * k + 1))
                ve.reciprocal(inverse, total).then_inc(soft_n, 1)
                ve.wait_ge(soft_n, due(soft_n, 6 * n + 3 * k + 2))
                ve.tensor_tensor(rows, rows, inverse.unsqueeze(2).to_broadcast([128, 2 * G, S]), ALU.mult)\
                    .then_inc(soft_n, 1)

            def add_up_last():
                b = B - 1
                ve.wait_ge(acc_done, due(acc_done, 2 * b * ADDS))
                for half in range(2):
                    dst = acc[:, b // 2 % 2, half * 8:(half + 1) * 8, b % 2 * SLOT:b % 2 * SLOT + S]
                    for k in range(1, ADDS + 1):
                        unit = (b * 2 + half) * 12 + k
                        ve.wait_ge(exp_done, due(exp_done, unit + 1))
                        if k == 1:
                            first = p_ring[:, (unit - 1) % PR, :].rearrange("p (h s) -> p h s", s=S)
                        else:
                            ve.wait_ge(acc_done, due(acc_done, (b * 2 + half) * ADDS + k - 1))
                            first = dst
                        ve.tensor_tensor(dst, first, p_ring[:, unit % PR, :].rearrange("p (h s) -> p h s", s=S),
                                         ALU.add).then_inc(acc_done, 1)

            def reduce_piece(b, p):
                unit = b * PIECES + p
                ve.wait_ge(mx_done, due(mx_done, unit + 1))
                ve.tensor_reduce(mx_p[:, p:p + 1], mx_ps[unit % MXB][:, 0:KP], AX.X, ALU.max).then_inc(red_done, 1)

            def negated_maxima(b):
                ve.wait_ge(red_done, due(red_done, (b + 1) * PIECES))
                ve.tensor_reduce(nm[:, :], mx_p[:, :].rearrange("p (j k) -> p j k", k=3), AX.X, ALU.max, negate=True)\
                    .then_inc(nm_step, 1)
                ve.wait_ge(nm_step, due(nm_step, 3 * b + 1))
                if b:
                    ve.wait_ge(ps["MT"], due(ps["MT"], b))
                ve.tensor_copy(nm_hl[:, 0, :], nm[:, :]).then_inc(nm_step, 1)
                ve.wait_ge(nm_step, due(nm_step, 3 * b + 2))
                ve.tensor_tensor(nm_hl[:, 1, :], nm[:, :], nm_hl[:, 0, :].bitcast(F32), ALU.subtract)\
                    .then_inc(nm_step, 1)

            ve.memset(x_sb[:, :, :], 0.0).then_inc(dve_c, 1)
            ve.memset(vhat[:, :, :, :], 0.0)
            ve.memset(eps_col[:, :], EPS)
            ve.memset(minus_half[:, :], -0.5).then_inc(dve_c, 1)
            step("L0", 0)
            step("N0", 0)
            ve.wait_ge(pool_c, due(pool_c, IDENT_MADE))
            ve.tensor_reduce(gmask[:, :], ident[:, :].rearrange("p (g d) -> p g d", d=HD), AX.X, ALU.add)
            ve.tensor_reduce(e8[:, :], ident[:, :].rearrange("p (a e) -> p e a", e=8), AX.X, ALU.add)\
                .then_inc(dve_c, 1)
            ve.wait_ge(dve_c, due(dve_c, 3))
            step("K", 0)
            ve.wait_ge(pool_c, due(pool_c, MASKS_MADE))
            for name in ("S0", "S1", "S2", "S3"):
                step(name, 0)
            ve.wait_ge(raw_in, due(raw_in, 16 * 3))
            ve.tensor_tensor(gkron[:, :, :], g8[:, :].unsqueeze(2).to_broadcast([128, PAIRS, 8]),
                             e8[:, :].unsqueeze(1).to_broadcast([128, PAIRS, 8]), ALU.mult).then_inc(dve_c, 1)
            for name in ("SM0", "SM1", "SN0", "SN1", "AS"):
                step(name, 0)
            for name in ("W1", "N1", "H0", "H1", "H2", "H3"):
                step(name, 0)

            def body(i):
                if i == PAIRS:
                    add_up_last()
                for g in range(2 * GROUPS):
                    part, gg = g // GROUPS, g % GROUPS
                    bm = 2 * i + part
                    if bm < B:
                        for p in pieces_within(g):
                            reduce_piece(bm, p)
                    for name, n in steps_of(i, g):
                        step(name, n, i, g)

            run_bodies(ve, at, body)

        @block.gpsimd
        def _(po):
            at = [None]
            due = counter(at)

            def add_up(b, half, since=1, until=ADDS):
                if 0 <= b < B:
                    base = (b * 2 + half) * ADDS
                    dst = acc[:, b // 2 % 2, half * 8:(half + 1) * 8, b % 2 * SLOT:b % 2 * SLOT + S]
                for k in range(since, until + 1):
                    if 0 <= b < B:
                        unit = (b * 2 + half) * 12 + k
                        po.wait_ge(exp_done, due(exp_done, unit + 1))
                        if k == 1:
                            first = p_ring[:, (unit - 1) % PR, :].rearrange("p (h s) -> p h s", s=S)
                        else:
                            po.wait_ge(acc_done, due(acc_done, base + k - 1))
                            first = dst
                        po.tensor_tensor(dst, first, p_ring[:, unit % PR, :].rearrange("p (h s) -> p h s", s=S),
                                         ALU.add).then_inc(acc_done, 1)

            def power(which, n):
                if not 0 <= n < PAIRS:
                    return
                po.wait_ge(ln[which], due(ln[which], (3 * n + 2, 4 * n + 3, 5 * n + 4)[which]))
                po.tensor_tensor(rstd[:, which, 0:1], mv[:, which, 1:2], eps_col[:, :], ALU.add)\
                    .then_inc(ln_eps[which], 1)
                po.wait_ge(ln_eps[which], due(ln_eps[which], n + 1))
                po.tensor_tensor(rstd[:, which, 1:2], rstd[:, which, 0:1], minus_half[:, :], ALU.pow)\
                    .then_inc(ln_pow[which], 1)

            made = [0]

            def make(instruction):
                made[0] += 1
                instruction.then_inc(pool_c, 1)
                po.wait_ge(pool_c, due(pool_c, made[0]))

            make(po.memset(ident[:, :], 0.0))
            make(po.affine_select(out=ident[:, :], in_=ident[:, :], compare_op=ALU.not_equal, fill=1.0,
                                  base=0, pattern=[[-1, 128]], channel_multiplier=1))
            assert made[0] == IDENT_MADE
            po.wait_ge(dve_c, due(dve_c, 2))
            power(0, 0)
            make(po.memset(cmask[:, :], 0.0))
            for h in range(2):
                half_mask = cmask[h * SLOT:(h + 1) * SLOT, :]
                make(po.affine_select(out=half_mask, in_=half_mask, compare_op=ALU.is_ge, fill=NEG, base=0,
                                      pattern=[[-1, S]], channel_multiplier=1))
            make(po.memset(p1[:, :, S:SLOT], 0.0))
            assert made[0] == MASKS_MADE
            make(po.memset(ones[:, :], 1.0))

            make(po.memset(y_t[:, :, :], 0.0))
            make(po.memset(ax_t[64:96, :], 1.0))
            make(po.memset(b_sb[64:96, :], 0.0))
            assert made[0] == PADS_MADE
            make(po.memset(c_st[96:98, :, :].bitcast(F32), 1.0))
            power(1, 0)
            po.wait_ge(eff_out, due(eff_out, 32))
            make(po.memset(acc[:, :, :, :], 1.0))
            assert made[0] == ALL_MADE

            def body(i):
                power(0, i + 1)
                if i < PAIRS:
                    for half in range(2):
                        add_up(2 * i - 1, half)
                add_up(2 * i, 0)
                power(1, i + 1)
                add_up(2 * i, 1, until=3)
                power(2, i - 1)
                add_up(2 * i, 1, since=4)

            run_bodies(po, at, body)


def kernel(**inputs):
    import numpy as np
    import concourse.bacc as bacc
    from concourse.bass_utils import run_bass_kernel_spmd

    a = {k: np.asarray(v) for k, v in inputs.items()}
    arrays = {
        "x": a["x"].reshape(PAIRS, 2, S, D),
        "ctx_t": a["ctx_4096"].transpose(0, 2, 1),
        "wq": a["L0_attn_wq"].reshape(D, G, R, HD).transpose(0, 2, 1, 3).reshape(D, D),
        "wk": a["L0_attn_wk"],
        "wv": a["L0_attn_wv"],
        "wo": a["L0_attn_wo"].reshape(G, R, HD, D).transpose(1, 0, 2, 3).reshape(D, D),
        "wq_d": a["L0_xattn_Wq_d"],
        "w_qk": a["L0_xattn_W_qk"],
        "wkv_d": a["L0_xattn_Wkv_d"],
        "wv_u": a["L0_xattn_Wv_u"],
        "gate_t": np.repeat(a["L0_ffn_gate"].transpose(1, 0), 8, axis=0),
        "kern": a["L0_ffn_kernel"],
        "bias": a["L0_ffn_bias"].reshape(1, D),
        "lora_a": a["L0_ffn_lora_A"].transpose(0, 2, 1),
        "lora_b": a["L0_ffn_lora_B"].transpose(0, 2, 1),
        "lora_as": a["L0_ffn_lora_A_shared"].transpose(1, 0),
        "lora_bs": a["L0_ffn_lora_B_shared"].transpose(1, 0),
    }
    nc = bacc.Bacc("TRN2", target_bir_lowering=False, num_devices=1, dynamic_dma_scratch_size=1024)
    ins, feed = {}, {}
    for name, value in arrays.items():
        value = np.ascontiguousarray(value)
        feed[f"in_{name}"] = value
        ins[name] = nc.dram_tensor(f"in_{name}", value.shape, mybir.dt.from_np(value.dtype), kind="ExternalInput").ap()
    out = nc.dram_tensor("out_y", (PAIRS, 2, S, D), F32, kind="ExternalOutput").ap()
    decoder_layer(nc, **ins, out=out)
    result = run_bass_kernel_spmd(nc, [feed], core_ids=[0])
    return result.results[0]["out_y"].reshape(B, S, D)
```
